# Optimizing a Trainium2 kernel written in Bass

```python
import numpy as np
import jax
import jax.numpy as jnp

def _softmax(x, axis=-1):
    return jax.nn.softmax(x, axis=axis)

def _gelu(x):
    return jax.nn.gelu(x, approximate=True)

def _silu(x):
    return jax.nn.silu(x)

def _sigmoid(x):
    return jax.nn.sigmoid(x)

def _layernorm(x, axis=-1, eps=1e-05):
    m = jnp.mean(x, axis=axis, keepdims=True)
    v = jnp.var(x, axis=axis, keepdims=True)
    return (x - m) / jnp.sqrt(v + eps)

def _scatter_add(tgt, idx, src, axis=0):
    return tgt.at[idx].add(src)

def _segment_sum(src, seg, n):
    return jax.ops.segment_sum(src, seg, n)
kernel_name = 'mk_vit_tower_d1_tok_img512_r4_7d5888'

def setup_inputs(seed: int=0):
    np.random.seed(seed)
    _w = jnp.asarray

    def _rec_inputs():
        import jax
        import jax.numpy as jnp
        _rk = jax.random.key(seed)
        x = -0.000222058 + 0.999998 * jax.random.normal(jax.random.fold_in(_rk, 1), (64, 3, 64, 64), jnp.float32)
        return x
    x = _rec_inputs()

    def _L0_tok_setup():
        import jax, jax.numpy as jnp
        import numpy as np
        IMG, P, C, D = (64, 16, 3, 128)
        NP = (IMG // P) ** 2
        PD = P * P * C
        key = jax.random.key(seed)
        k1, k2, k3 = jax.random.split(key, 3)
        x = jax.random.normal(k1, (128, C, IMG, IMG), dtype=jnp.float32)
        W = jax.random.normal(k2, (D, PD), dtype=jnp.float32) * (1.0 / np.sqrt(PD))
        b = jax.random.normal(k3, (D,), dtype=jnp.float32) * 0.01
        return {'x': x, 'W': W, 'b': b}
    _L0_tok_all = _L0_tok_setup()
    _L0_tok_in = {k: v for k, v in _L0_tok_all.items() if k in ('W', 'b')}
    del _L0_tok_all

    def _L0_attn_setup():
        import jax, jax.numpy as jnp
        import numpy as np
        D_MODEL = 128
        N_HEADS = 8
        D_HEAD = D_MODEL // N_HEADS
        SCALE = 1.0 / np.sqrt(D_MODEL).astype(np.float32)
        key = jax.random.key(seed)
        ks = jax.random.split(key, 9)
        B, S = (4, 512)
        std = 1.0 / np.sqrt(D_MODEL).astype(np.float32)
        x = jax.random.normal(ks[0], (B, S, D_MODEL), dtype=jnp.float32)
        Wq = jax.random.normal(ks[1], (D_MODEL, D_MODEL), dtype=jnp.float32) * std
        bq = jnp.zeros((D_MODEL,), jnp.float32)
        Wk = jax.random.normal(ks[2], (D_MODEL, D_MODEL), dtype=jnp.float32) * std
        bk = jnp.zeros((D_MODEL,), jnp.float32)
        Wv = jax.random.normal(ks[3], (D_MODEL, D_MODEL), dtype=jnp.float32) * std
        bv = jnp.zeros((D_MODEL,), jnp.float32)
        Wo = jax.random.normal(ks[4], (D_MODEL, D_MODEL), dtype=jnp.float32) * std
        bo = jnp.zeros((D_MODEL,), jnp.float32)
        return {'x': x, 'Wq': Wq, 'bq': bq, 'Wk': Wk, 'bk': bk, 'Wv': Wv, 'bv': bv, 'Wo': Wo, 'bo': bo}
    _L0_attn_all = _L0_attn_setup()
    _L0_attn_in = {k: v for k, v in _L0_attn_all.items() if k in ('Wq', 'bq', 'Wk', 'bk', 'Wv', 'bv', 'Wo', 'bo')}
    del _L0_attn_all

    def _L0_ffn_setup():
        import jax, jax.numpy as jnp
        import numpy as np
        D = 128
        E = 8
        K = 2
        EXP = 4
        LN_EPS = 1e-05
        key = jax.random.key(seed)
        ks = jax.random.split(key, 8)
        B, T = (8, 512)
        Dh = D * EXP
        x = jax.random.normal(ks[0], (B, T, D), dtype=jnp.float32)
        ln_g = jnp.ones((D,), dtype=jnp.float32)
        ln_b = jnp.zeros((D,), dtype=jnp.float32)
        lim_r = np.sqrt(6.0 / (D + E)).astype(np.float32)
        w_r = jax.random.uniform(ks[1], (E, D), dtype=jnp.float32, minval=-lim_r, maxval=lim_r)
        b_r = jnp.zeros((E,), dtype=jnp.float32)
        lim1 = np.sqrt(6.0 / (D + Dh)).astype(np.float32)
        W1 = jax.random.uniform(ks[2], (E, D, Dh), dtype=jnp.float32, minval=-lim1, maxval=lim1)
        b1 = jnp.zeros((E, Dh), dtype=jnp.float32)
        W2 = jax.random.uniform(ks[3], (E, Dh, D), dtype=jnp.float32, minval=-lim1, maxval=lim1)
        b2 = jnp.zeros((E, D), dtype=jnp.float32)
        return {'x': x, 'ln_g': ln_g, 'ln_b': ln_b, 'w_r': w_r, 'b_r': b_r, 'W1': W1, 'b1': b1, 'W2': W2, 'b2': b2}
    _L0_ffn_all = _L0_ffn_setup()
    _L0_ffn_in = {k: v for k, v in _L0_ffn_all.items() if k in ('ln_g', 'ln_b', 'w_r', 'b_r', 'W1', 'b1', 'W2', 'b2')}
    del _L0_ffn_all
    return {'x': x, 'L0_tok_W': _L0_tok_in['W'], 'L0_tok_b': _L0_tok_in['b'], 'L0_attn_Wq': _L0_attn_in['Wq'], 'L0_attn_bq': _L0_attn_in['bq'], 'L0_attn_Wk': _L0_attn_in['Wk'], 'L0_attn_bk': _L0_attn_in['bk'], 'L0_attn_Wv': _L0_attn_in['Wv'], 'L0_attn_bv': _L0_attn_in['bv'], 'L0_attn_Wo': _L0_attn_in['Wo'], 'L0_attn_bo': _L0_attn_in['bo'], 'L0_ffn_ln_g': _L0_ffn_in['ln_g'], 'L0_ffn_ln_b': _L0_ffn_in['ln_b'], 'L0_ffn_w_r': _L0_ffn_in['w_r'], 'L0_ffn_b_r': _L0_ffn_in['b_r'], 'L0_ffn_W1': _L0_ffn_in['W1'], 'L0_ffn_b1': _L0_ffn_in['b1'], 'L0_ffn_W2': _L0_ffn_in['W2'], 'L0_ffn_b2': _L0_ffn_in['b2']}

def reference(x, L0_tok_W, L0_tok_b, L0_attn_Wq, L0_attn_bq, L0_attn_Wk, L0_attn_bk, L0_attn_Wv, L0_attn_bv, L0_attn_Wo, L0_attn_bo, L0_ffn_ln_g, L0_ffn_ln_b, L0_ffn_w_r, L0_ffn_b_r, L0_ffn_W1, L0_ffn_b1, L0_ffn_W2, L0_ffn_b2):
    import jax
    import jax.numpy as jnp

    def _L0_tok_ref(x, W, b):
        import jax, jax.numpy as jnp
        import numpy as np
        IMG, P, C, D = (64, 16, 3, 128)
        NP = (IMG // P) ** 2
        PD = P * P * C
        B, c, H, Wd = x.shape
        xp = x.reshape(B, c, H // P, P, Wd // P, P)
        xp = xp.transpose(0, 2, 4, 1, 3, 5).reshape(B, NP, c * P * P)
        return jnp.einsum('bnk,dk->bnd', xp, W) + b

    def _L0_attn_ref(x, Wq, bq, Wk, bk, Wv, bv, Wo, bo):
        import jax, jax.numpy as jnp
        import numpy as np
        D_MODEL = 128
        N_HEADS = 8
        D_HEAD = D_MODEL // N_HEADS
        SCALE = 1.0 / np.sqrt(D_MODEL).astype(np.float32)
        B, S, _ = x.shape

        def split_heads(t):
            return t.reshape(B, S, N_HEADS, D_HEAD).transpose(0, 2, 1, 3)
        q = split_heads(x @ Wq + bq)
        k = split_heads(x @ Wk + bk)
        v = split_heads(x @ Wv + bv)
        scores = jnp.einsum('bhqd,bhkd->bhqk', q, k) * SCALE
        weights = jax.nn.softmax(scores, axis=-1)
        att = jnp.einsum('bhqk,bhkd->bhqd', weights, v)
        att = att.transpose(0, 2, 1, 3).reshape(B, S, D_MODEL)
        return att @ Wo + bo

    def _L0_ffn_ref(x, ln_g, ln_b, w_r, b_r, W1, b1, W2, b2):
        import jax, jax.numpy as jnp
        import numpy as np
        D = 128
        E = 8
        K = 2
        EXP = 4
        LN_EPS = 1e-05
        B, T, d = x.shape
        mu = jnp.mean(x, axis=-1, keepdims=True)
        var = jnp.mean(jnp.square(x - mu), axis=-1, keepdims=True)
        h = (x - mu) * jax.lax.rsqrt(var + LN_EPS) * ln_g + ln_b
        logits = jnp.einsum('btd,ed->bte', h, w_r) + b_r
        topk_vals, topk_idx = jax.lax.top_k(logits, K)
        gates = jax.nn.softmax(topk_vals, axis=-1)
        hf = h.reshape(B * T, d)
        hid = jax.nn.gelu(jnp.einsum('nd,edf->nef', hf, W1) + b1, approximate=False)
        expert_stack = jnp.einsum('nef,efd->ned', hid, W2) + b2
        idx_flat = topk_idx.reshape(B * T, K)
        gates_flat = gates.reshape(B * T, K)
        gathered = jnp.take_along_axis(expert_stack, idx_flat[:, :, None], axis=1)
        mixed = jnp.sum(gathered * gates_flat[:, :, None], axis=1).reshape(B, T, d)
        return x + mixed
    h = _L0_tok_ref(x, L0_tok_W, L0_tok_b)
    h = h + _L0_attn_ref(_layernorm(h, axis=-1), L0_attn_Wq, L0_attn_bq, L0_attn_Wk, L0_attn_bk, L0_attn_Wv, L0_attn_bv, L0_attn_Wo, L0_attn_bo)
    h = h + _L0_ffn_ref(_layernorm(h, axis=-1), L0_ffn_ln_g, L0_ffn_ln_b, L0_ffn_w_r, L0_ffn_b_r, L0_ffn_W1, L0_ffn_b1, L0_ffn_W2, L0_ffn_b2)
    return h

_drawn_inputs = setup_inputs


def setup_inputs(seed=0):
    import zlib

    import numpy as np

    out = dict(_drawn_inputs(seed))
    spreads = {'L0_attn_bq': (0.0, 0.638),
     'L0_attn_bk': (0.0, 0.8),
     'L0_attn_bv': (0.0, 0.1),
     'L0_attn_bo': (0.0, 0.1),
     'L0_ffn_ln_g': (1.0, 0.2),
     'L0_ffn_ln_b': (0.0, 0.1),
     'L0_ffn_b_r': (0.0, 0.1),
     'L0_ffn_b1': (0.0, 0.27),
     'L0_ffn_b2': (0.0, 0.1)}
    factors = {'L0_tok_b': 2.675}
    for name, (base, spread) in spreads.items():
        noise = np.random.default_rng([zlib.crc32(name.encode()), seed]).standard_normal(out[name].shape)
        drawn = base * np.exp(spread * noise) if base else spread * noise
        out[name] = jnp.asarray(drawn.astype(out[name].dtype))
    for name, factor in factors.items():
        out[name] = (out[name] * factor).astype(out[name].dtype)
    return out
```

```python
from contextlib import ExitStack

import concourse.bass as bass
from concourse import mybir

BATCH, CHANNELS, IMG, PATCH, D = 64, 3, 64, 16, 128
SEQ = (IMG // PATCH) ** 2
TOKENS = BATCH * SEQ
PATCH_DIM = CHANNELS * PATCH * PATCH
HEADS = 8
DH = D // HEADS
EXPERTS, HID = 8, 512
EPS = 1e-5
SCALE = 1.0 / float(D) ** 0.5

P = 128
KC = PATCH_DIM // P
FC = HID // P
GROUPS = TOKENS // P
HALVES = 2
HG = GROUPS // HALVES
HT = TOKENS // HALVES
IPG = P // SEQ
HI = BATCH // HALVES
QKV_BANKS = ((3, 4, 5), (6, 7, 0))
HID_BANKS = (7, 1, 3)
OUT_BANKS = (4, 0)
DVE_SHARE = 5
NMIN = 96


def vit_tower(nc, x_t, w_tok, w_attn, rows, cols, w_router, b_router, w1, b1, w2, b2, out):
    fp32 = mybir.dt.float32
    ALU = mybir.AluOpType
    ACT = mybir.ActivationFunctionType
    AX = mybir.AxisListType.X

    with ExitStack() as ctx:
        def sb(name, shape):
            return ctx.enter_context(nc.sbuf_tensor(name, shape, fp32))

        def sem(name):
            return ctx.enter_context(nc.semaphore(name))

        x_sb = sb("x_sb", [P, GROUPS, KC, P])
        wtok_sb = sb("wtok_sb", [P, KC, D])
        wqkvo = sb("wqkvo", [P, 4, D])
        rows_sb = sb("rows_sb", [P, 3, D])
        cols_sb = sb("cols_sb", [P, 4])
        wr_sb = sb("wr_sb", [P, EXPERTS])
        br_sb = sb("br_sb", [P, EXPERTS])
        w1_sb = sb("w1_sb", [P, EXPERTS, HID])
        w2_sb = sb("w2_sb", [P, EXPERTS, FC, D])
        b1_sb = sb("b1_sb", [P, EXPERTS * FC])
        b2_blk = sb("b2_blk", [HG * EXPERTS, HG, D])
        ident = sb("ident", [P, P])
        mask16 = sb("mask16", [P, IPG])
        pick = sb("pick", [P, EXPERTS])
        minus_half = sb("minus_half", [P, HG])
        h_sb = sb("h_sb", [P, GROUPS, D])
        hbo_sb = sb("hbo_sb", [P, GROUPS, D])
        z_sb = sb("z_sb", [P, GROUPS, D])
        n_sb = sb("n_sb", [P, GROUPS, D])
        acc = sb("acc", [P, GROUPS, D])
        y_t = sb("y_t", [P, HALVES, HT])
        q_t = sb("q_t", [P, HALVES, HT])
        k_t = sb("k_t", [P, HALVES, HT])
        spread = sb("spread", [P, HALVES, HI * HEADS * SEQ])
        q_bd = spread[:].rearrange("p n (i h s) -> p n i h s", h=HEADS, s=SEQ)
        p_bd = spread[:].rearrange("p n (g h i s) -> p n g h i s", h=HEADS, i=IPG, s=SEQ)
        v_pad = sb("v_pad", [P, HALVES, HG, HEADS, D])
        e_sb = sb("e_sb", [P, HALVES, HI, SEQ])
        pt_sb = sb("pt_sb", [P, HALVES, HG * HEADS, SEQ])
        att_t = sb("att_t", [P, HALVES, HT])
        hh_t = sb("hh_t", [P, HALVES, HT])
        hid = sb("hid", [P, 2, FC, HT])
        st6 = sb("st6", [P, HG, 6])
        mv = sb("mv", [P, HG, 2])
        veps = sb("veps", [P, HG])
        r0 = sb("r0", [P, HG])
        r1 = sb("r1", [P, HG])
        rstd = sb("rstd", [P, HG])
        mx = sb("mx", [P, HALVES, HI])
        sm = sb("sm", [P, HALVES, HI])
        rs = sb("rs", [P, HALVES, HI])
        lg = sb("lg", [P, HG, EXPERTS])
        t8 = sb("t8", [P, HG, EXPERTS])
        oh = sb("oh", [P, HALVES, 2, HG, EXPERTS])
        top = sb("top", [P, HALVES, 2, HG])
        tmax = sb("tmax", [P, HG])
        gd = sb("gd", [P, HALVES, HG])
        gate = sb("gate", [P, HALVES, 2, HG])
        lg2 = sb("lg2", [P, HALVES, HG, EXPERTS])
        G = sb("G", [P, HALVES, HG, EXPERTS])
        g_t = sb("g_t", [HG * EXPERTS, HALVES, P])

        bank = [ctx.enter_context(nc.psum_tensor(f"bank{i}", [P, HT], fp32)) for i in range(8)]

        def spread_out(half, i):
            return p_bd[:, half, :, :, i].rearrange("p g h s -> p (g h) s")

        def v_diagonal(half, j):
            rows_ = v_pad[:, half, j].rearrange("p h d -> p (h d)")
            return bass.AP(tensor=rows_.tensor, offset=rows_.offset, ap=[rows_.ap[0], [D + DH, HEADS], [1, DH]])

        s_x = [sem(f"s_x{g}") for g in range(GROUPS)]
        s_w1 = [sem(f"s_w1_{e}") for e in range(EXPERTS)]
        s_w2 = [sem(f"s_w2_{e}") for e in range(EXPERTS)]
        (s_wtok, s_wattn, s_rows, s_cols, s_router, s_b1, s_b2) = (
            sem(n) for n in ("s_wtok", "s_wattn", "s_rows", "s_cols", "s_router", "s_b1", "s_b2"))
        (s_const, s_pool, s_vzero, s_dve) = (sem(n) for n in ("s_const", "s_pool", "s_vzero", "s_dve"))
        (s_patch, s_h, s_hbo, s_var, s_pow, s_norm, s_tr, s_yt) = (
            sem(n) for n in ("s_patch", "s_h", "s_hbo", "s_var", "s_pow", "s_norm", "s_tr", "s_yt"))
        (s_qkv, s_qt, s_kt, s_vp, s_qbd, s_qbda, s_sc, s_sub, s_exp, s_p) = (
            sem(n) for n in ("s_qkv", "s_qt", "s_kt", "s_vp", "s_qbd", "s_qbda", "s_sc", "s_sub", "s_exp", "s_p"))
        (s_pT, s_ptc, s_pbd, s_pbda, s_pv, s_at, s_o, s_z) = (
            sem(n) for n in ("s_pT", "s_ptc", "s_pbd", "s_pbda", "s_pv", "s_at", "s_o", "s_z"))
        (s_hht, s_lg, s_gdiff, s_gexp, s_G, s_gT, s_gtc, s_b2y, s_hz) = (
            sem(n) for n in ("s_hht", "s_lg", "s_gdiff", "s_gexp", "s_G", "s_gT", "s_gtc", "s_b2y", "s_hz"))
        (s_hid, s_gelu, s_y, s_acc, s_out) = (sem(n) for n in ("s_hid", "s_gelu", "s_y", "s_acc", "s_out"))

        block = ctx.enter_context(nc.Block())

        @block.sync
        def _(sp):
            sp.dma_start(wtok_sb[:], w_tok).then_inc(s_wtok, 16)
            for g in range(GROUPS):
                sp.dma_start(x_sb[:, g], x_t[:, g]).then_inc(s_x[g], 16)
                if g == 3:
                    sp.dma_start(wqkvo[:], w_attn).then_inc(s_wattn, 16)
            for e in range(EXPERTS):
                sp.dma_start(w1_sb[:, e], w1[:, e]).then_inc(s_w1[e], 16)
                sp.dma_start(w2_sb[:, e], w2[:, e]).then_inc(s_w2[e], 16)
            for half in range(HALVES):
                sp.wait_ge(s_acc, HALVES + EXPERTS * (half + 1))
                sp.dma_start(out[:, half * HG:(half + 1) * HG], acc[:, half * HG:(half + 1) * HG]).then_inc(s_out, 16)
            sp.wait_ge(s_out, 16 * HALVES)

        @block.gpsimd
        def _(pool):
            nc.gpsimd.memset(ident[:], 0.0).then_inc(s_pool, 1)
            nc.gpsimd.memset(mask16[:], 1.0).then_inc(s_pool, 1)
            nc.gpsimd.memset(minus_half[:], -0.5).then_inc(s_const, 1)
            nc.gpsimd.memset(b2_blk[:], 0.0).then_inc(s_const, 1)
            nc.gpsimd.iota(pick[:], pattern=[[-1, EXPERTS]], base=EXPERTS, channel_multiplier=0,
                           allow_small_or_imprecise_dtypes=True).then_inc(s_const, 1)
            pool.wait_ge(s_pool, 2)
            nc.gpsimd.affine_select(out=ident[:], in_=ident[:], compare_op=ALU.not_equal, fill=1.0, base=0,
                                    pattern=[[-1, P]], channel_multiplier=1).then_inc(s_const, 1)
            nc.gpsimd.affine_select(out=mask16[:], in_=mask16[:], compare_op=ALU.is_ge, fill=0.0, base=0,
                                    pattern=[[-SEQ, IPG]], channel_multiplier=1).then_inc(s_pool, 1)
            pool.wait_ge(s_pool, 3)
            nc.gpsimd.affine_select(out=mask16[:], in_=mask16[:], compare_op=ALU.is_ge, fill=0.0, base=SEQ - 1,
                                    pattern=[[SEQ, IPG]], channel_multiplier=-1).then_inc(s_const, 1)
            pool.wait_ge(s_const, 5)
            for g in range(HG):
                pool.dma_start(b2_blk[g * EXPERTS:(g + 1) * EXPERTS, g], b2).then_inc(s_b2, 16)
            nc.gpsimd.memset(v_pad[:, 1], 0.0).then_inc(s_vzero, 1)

            def power(n):
                pool.wait_ge(s_var, n + 1)
                nc.gpsimd.tensor_tensor(r0[:], veps[:], minus_half[:], ALU.pow).then_inc(s_pow, 1)

            for half in range(HALVES):
                power(half)
            pool.wait_ge(s_rows, 16)
            for half in range(HALVES):
                pool.wait_ge(s_h, half + 1)
                hs = slice(half * HG, (half + 1) * HG)
                nc.gpsimd.tensor_tensor(hbo_sb[:, hs], h_sb[:, hs], rows_sb[:, 2:3].to_broadcast([P, HG, D]),
                                        ALU.add).then_inc(s_hbo, 1)
            for half in range(HALVES):
                power(HALVES + 2 * half)
                power(HALVES + 2 * half + 1)
            for half in range(HALVES):
                pool.wait_ge(s_z, half + 1)
                hs = slice(half * HG, (half + 1) * HG)
                nc.gpsimd.tensor_tensor(acc[:, hs], h_sb[:, hs], z_sb[:, hs], ALU.add).then_inc(s_hz, 1)

        @block.tensor
        def _(pe):
            def patches(half):
                for j in range(HG):
                    g = half * HG + j
                    pe.wait_ge(s_x[g], 16)
                    for c in range(KC):
                        last = nc.tensor.matmul(bank[half][:, j * D:(j + 1) * D], x_sb[:, g, c], wtok_sb[:, c],
                                                start=(c == 0), stop=(c == KC - 1))
                    last.then_inc(s_patch, 1)

            def transposes(to, src, done):
                for j in range(HG):
                    last = nc.tensor.transpose(to[:, j * P:(j + 1) * P], src(j), ident[:])
                last.then_inc(done, 1)

            def qkv(half):
                q_bank, k_bank, v_bank = QKV_BANKS[half]
                pe.wait_ge(s_yt, half + 1)
                nc.tensor.matmul(bank[q_bank][:], wqkvo[:, 0], y_t[:, half], start=True, stop=True).then_inc(s_qkv, 1)
                nc.tensor.matmul(bank[k_bank][:], wqkvo[:, 1], y_t[:, half], start=True, stop=True).then_inc(s_qkv, 1)
                for j in range(HG):
                    last = nc.tensor.matmul(bank[v_bank][:, j * D:(j + 1) * D], y_t[:, half, j * P:(j + 1) * P],
                                            wqkvo[:, 2], start=True, stop=True)
                last.then_inc(s_qkv, 1)

            def scores(half):
                pe.wait_ge(s_qbd, DVE_SHARE * (half + 1))
                pe.wait_ge(s_qbda, (HEADS - DVE_SHARE) * (half + 1))
                pe.wait_ge(s_kt, half + 1)
                for i in range(HI):
                    at = i * SEQ
                    n = NMIN if at + NMIN <= HT else SEQ
                    last = nc.tensor.matmul(bank[1 + half][:, at:at + n], q_bd[:, half, i].rearrange("p h s -> p (h s)"),
                                            k_t[:, half, at:at + n], start=True, stop=True)
                last.then_inc(s_sc, 1)

            def weighted(half):
                pe.wait_ge(s_pbd, DVE_SHARE * (half + 1))
                pe.wait_ge(s_pbda, (IPG - DVE_SHARE) * (half + 1))
                pe.wait_ge(s_vp, half + 1)
                for j in range(HG):
                    for hd in range(HEADS):
                        last = nc.tensor.matmul(bank[5 + half][:, j * P:(j + 1) * P], v_pad[:, half, j, hd],
                                                p_bd[:, half, j, hd].rearrange("p i s -> p (i s)"),
                                                start=(hd == 0), stop=(hd == HEADS - 1))
                last.then_inc(s_pv, 1)

            def project(half):
                pe.wait_ge(s_at, half + 1)
                for j in range(HG):
                    last = nc.tensor.matmul(bank[(7, 0)[half]][:, j * D:(j + 1) * D], att_t[:, half, j * P:(j + 1) * P],
                                            wqkvo[:, 3], start=True, stop=True)
                last.then_inc(s_o, 1)

            def router(half):
                pe.wait_ge(s_hht, half + 1)
                for j in range(HG):
                    last = nc.tensor.matmul(bank[5 + half][:, j * EXPERTS:(j + 1) * EXPERTS],
                                            hh_t[:, half, j * P:(j + 1) * P], wr_sb[:], start=True, stop=True)
                last.then_inc(s_lg, 1)

            def bias2(half):
                pe.wait_ge(s_G, half + 1)
                nc.tensor.transpose(bank[5 + half][0:HG * EXPERTS, 0:P],
                                    G[:, half].rearrange("p g e -> p (g e)"), ident[:]).then_inc(s_gT, 1)
                pe.wait_ge(s_gtc, half + 1)
                nc.tensor.matmul(bank[5 + half][:], g_t[:, half], b2_blk[:].rearrange("p g d -> p (g d)"),
                                 start=True, stop=True).then_inc(s_b2y, 1)

            def up(n):
                half, e = divmod(n, EXPERTS)
                if half == 0:
                    pe.wait_ge(s_w1[e], 16)
                for c in range(FC):
                    m = n * FC + c
                    if m >= len(HID_BANKS):
                        pe.wait_ge(s_gelu, m - len(HID_BANKS) + 1)
                    nc.tensor.matmul(bank[HID_BANKS[m % len(HID_BANKS)]][:], w1_sb[:, e, c * P:(c + 1) * P],
                                     hh_t[:, half], start=True, stop=True).then_inc(s_hid, 1)

            def down(n):
                half, e = divmod(n, EXPERTS)
                if half == 0:
                    pe.wait_ge(s_w2[e], 16)
                pe.wait_ge(s_gelu, FC * (n + 1))
                if n >= 2:
                    pe.wait_ge(s_acc, HALVES + n - 1)
                for j in range(HG):
                    for c in range(FC):
                        last = nc.tensor.matmul(bank[OUT_BANKS[n % 2]][:, j * D:(j + 1) * D],
                                                hid[:, n % 2, c, j * P:(j + 1) * P],
                                                w2_sb[:, e, c], start=(c == 0), stop=(c == FC - 1))
                last.then_inc(s_y, 1)

            def rows_of(half):
                return lambda j: n_sb[:, half * HG + j]

            def weights_of(half):
                return lambda j: e_sb[:, half, j * IPG:(j + 1) * IPG].rearrange("p i s -> p (i s)")

            pe.wait_ge(s_wtok, 16)
            patches(0)
            patches(1)
            pe.wait_ge(s_const, 5)
            pe.wait_ge(s_wattn, 16)
            for half in range(HALVES):
                pe.wait_ge(s_norm, half + 1)
                if half:
                    pe.wait_ge(s_yt, half)
                transposes(bank[2], rows_of(half), s_tr)
                qkv(half)
            for half in range(HALVES):
                if half:
                    pe.wait_ge(s_yt, HALVES)
                scores(half)
            for half in range(HALVES):
                pe.wait_ge(s_p, half + 1)
                transposes(bank[3 + half], weights_of(half), s_pT)
            for half in range(HALVES):
                pe.wait_ge(s_vp, 1)
                pe.wait_ge(s_qt, HALVES)
                weighted(half)
                pe.wait_ge(s_kt, HALVES)
                pe.wait_ge(s_vp, HALVES)
                project(half)
            pe.wait_ge(s_router, 32)
            for half in range(HALVES):
                pe.wait_ge(s_norm, HALVES + half + 1)
                transposes(bank[1 + half], rows_of(half), s_tr)
                router(half)
                if half == 0:
                    up(0)
                    up(1)
            pe.wait_ge(s_b2, 16 * HG)
            bias2(0)
            bias2(1)
            last_n = HALVES * EXPERTS - 1
            down(0)
            for n in range(2, last_n + 1):
                up(n)
                down(n - 1)
            down(last_n)

        @block.scalar
        def _(act):
            act.dma_start(rows_sb[:], rows).then_inc(s_rows, 16)
            act.dma_start(cols_sb[:], cols).then_inc(s_cols, 16)
            act.dma_start(wr_sb[:], w_router).then_inc(s_router, 16)
            act.dma_start(br_sb[:], b_router).then_inc(s_router, 16)
            act.dma_start(b1_sb[:], b1).then_inc(s_b1, 16)
            act.wait_ge(s_cols, 16)
            act.wait_ge(s_const, 5)
            for half in range(HALVES):
                q_bank, k_bank, _ = QKV_BANKS[half]
                act.wait_ge(s_tr, half + 1)
                nc.scalar.activation(y_t[:, half], bank[2][:], ACT.Identity).then_inc(s_yt, 1)
                act.wait_ge(s_qkv, 3 * half + 1)
                nc.scalar.activation(q_t[:, half], bank[q_bank][:], ACT.Identity, bias=cols_sb[:, 0:1]).then_inc(s_qt, 1)
                act.wait_ge(s_qkv, 3 * half + 2)
                nc.scalar.activation(k_t[:, half], bank[k_bank][:], ACT.Identity, bias=cols_sb[:, 1:2]).then_inc(s_kt, 1)
                act.wait_ge(s_qt, half + 1)
                for hd in range(DVE_SHARE, HEADS):
                    nc.scalar.activation(q_bd[:, half, :, hd], q_t[:, half].rearrange("p (i s) -> p i s", s=SEQ),
                                         ACT.Copy, scale=mask16[:, hd:hd + 1]).then_inc(s_qbda, 1)
            for half in range(HALVES):
                act.wait_ge(s_sub, half + 1)
                nc.scalar.activation(e_sb[:, half], e_sb[:, half], ACT.Exp, scale=SCALE).then_inc(s_exp, 1)
            for half in range(HALVES):
                act.wait_ge(s_ptc, half + 1)
                for i in range(DVE_SHARE, IPG):
                    nc.scalar.activation(spread_out(half, i), pt_sb[:, half], ACT.Copy,
                                         scale=mask16[:, i:i + 1]).then_inc(s_pbda, 1)
            for half in range(HALVES):
                act.wait_ge(s_pv, half + 1)
                nc.scalar.activation(att_t[:, half], bank[5 + half][:], ACT.Identity).then_inc(s_at, 1)

            def to_hidden(half):
                act.wait_ge(s_tr, HALVES + half + 1)
                nc.scalar.activation(hh_t[:, half], bank[1 + half][:], ACT.Identity, scale=cols_sb[:, 2:3],
                                     bias=cols_sb[:, 3:4]).then_inc(s_hht, 1)

            def gelu(n):
                e = n % EXPERTS
                if n >= 2:
                    act.wait_ge(s_y, n - 1)
                for c in range(FC):
                    m = n * FC + c
                    act.wait_ge(s_hid, m + 1)
                    nc.scalar.activation(hid[:, n % 2, c], bank[HID_BANKS[m % len(HID_BANKS)]][:], ACT.Gelu,
                                         bias=b1_sb[:, e * FC + c:e * FC + c + 1]).then_inc(s_gelu, 1)

            to_hidden(0)
            act.wait_ge(s_b1, 16)
            gelu(0)
            gelu(1)
            to_hidden(1)
            for half in range(HALVES):
                act.wait_ge(s_gdiff, half + 1)
                nc.scalar.activation(gate[:, half, 1], gd[:, half], ACT.Exp).then_inc(s_gexp, 1)
            for half in range(HALVES):
                act.wait_ge(s_gT, half + 1)
                nc.scalar.activation(g_t[:, half], bank[5 + half][0:HG * EXPERTS, 0:P], ACT.Identity).then_inc(s_gtc, 1)
            for n in range(2, HALVES * EXPERTS):
                gelu(n)

        @block.vector
        def _(dve):
            chain = [0]

            def link(ins):
                chain[0] += 1
                ins.then_inc(s_dve, 1)
                dve.wait_ge(s_dve, chain[0])

            def statistics(src, half, n):
                for j in range(HG):
                    last = nc.vector.bn_stats(st6[:, j], src[:, half * HG + j])
                link(last)
                for j in range(HG):
                    last = nc.vector.bn_aggr(mv[:, j], st6[:, j])
                link(last)
                nc.vector.tensor_scalar(veps[:], mv[:, :, 1], EPS, None, ALU.add).then_inc(s_var, 1)
                dve.wait_ge(s_pow, n + 1)
                link(nc.vector.tensor_tensor(r1[:], r0[:], r0[:], ALU.mult))
                link(nc.vector.tensor_tensor(r1[:], r1[:], veps[:], ALU.mult))
                link(nc.vector.tensor_scalar(r1[:], r1[:], -0.5, 1.5, ALU.mult, ALU.add))
                link(nc.vector.tensor_tensor(rstd[:], r0[:], r1[:], ALU.mult))

            def normalise(dst, src, half, done):
                for j in range(HG):
                    g = half * HG + j
                    last = nc.vector.tensor_scalar(dst[:, g], src[:, g], mv[:, j, 0:1], rstd[:, j:j + 1],
                                                   ALU.subtract, ALU.mult)
                last.then_inc(done, 1)

            def spread_q(half):
                dve.wait_ge(s_qt, half + 1)
                for hd in range(DVE_SHARE):
                    nc.vector.tensor_scalar(q_bd[:, half, :, hd], q_t[:, half].rearrange("p (i s) -> p i s", s=SEQ),
                                            mask16[:, hd:hd + 1], None, ALU.mult).then_inc(s_qbd, 1)

            def spread_v(half):
                dve.wait_ge(s_qkv, 3 * half + 3)
                for j in range(HG):
                    nc_last = nc.vector.tensor_tensor(
                        v_diagonal(half, j), bank[QKV_BANKS[half][2]][:, j * D:(j + 1) * D].rearrange("p (h d) -> p h d", d=DH),
                        rows_sb[:, 1].rearrange("p (h d) -> p h d", d=DH), ALU.add)
                nc_last.then_inc(s_vp, 1)

            nc.vector.memset(v_pad[:, 0], 0.0).then_inc(s_vzero, 1)
            dve.wait_ge(s_rows, 16)
            for half in range(HALVES):
                hs = slice(half * HG, (half + 1) * HG)
                dve.wait_ge(s_patch, HG * (half + 1))
                nc.vector.tensor_tensor(h_sb[:, hs], bank[half][:].rearrange("p (g d) -> p g d", d=D),
                                        rows_sb[:, 0:1].to_broadcast([P, HG, D]), ALU.add).then_inc(s_h, 1)
                dve.wait_ge(s_h, half + 1)
                statistics(h_sb, half, half)
                normalise(n_sb, h_sb, half, s_norm)
            dve.wait_ge(s_const, 5)
            dve.wait_ge(s_vzero, 2)
            for half in range(HALVES):
                spread_q(half)
                spread_v(half)

            for half in range(HALVES):
                sc = bank[1 + half][:].rearrange("p (i s) -> p i s", s=SEQ)
                dve.wait_ge(s_sc, half + 1)
                link(nc.vector.tensor_reduce(mx[:, half], sc, AX, ALU.max))
                nc.vector.tensor_tensor(e_sb[:, half], sc, mx[:, half].unsqueeze(2).to_broadcast([P, HI, SEQ]),
                                        ALU.subtract).then_inc(s_sub, 1)
            for half in range(HALVES):
                dve.wait_ge(s_exp, half + 1)
                link(nc.vector.tensor_reduce(sm[:, half], e_sb[:, half], AX, ALU.add))
                link(nc.vector.reciprocal(rs[:, half], sm[:, half]))
                nc.vector.tensor_tensor(e_sb[:, half], e_sb[:, half], rs[:, half].unsqueeze(2).to_broadcast([P, HI, SEQ]),
                                        ALU.mult).then_inc(s_p, 1)
            for half in range(HALVES):
                dve.wait_ge(s_pT, half + 1)
                nc.vector.tensor_copy(pt_sb[:, half].rearrange("p a b -> p (a b)"), bank[3 + half][:]).then_inc(s_ptc, 1)
                dve.wait_ge(s_ptc, half + 1)
                for i in range(DVE_SHARE):
                    nc.vector.tensor_scalar(spread_out(half, i), pt_sb[:, half], mask16[:, i:i + 1], None,
                                            ALU.mult).then_inc(s_pbd, 1)

            for half in range(HALVES):
                hs = slice(half * HG, (half + 1) * HG)
                dve.wait_ge(s_hbo, half + 1)
                dve.wait_ge(s_o, half + 1)
                link(nc.vector.tensor_tensor(h_sb[:, hs], bank[(7, 0)[half]][:].rearrange("p (g d) -> p g d", d=D),
                                             hbo_sb[:, hs], ALU.add))
                statistics(h_sb, half, HALVES + 2 * half)
                normalise(z_sb, h_sb, half, s_z)
                dve.wait_ge(s_z, half + 1)
                statistics(z_sb, half, HALVES + 2 * half + 1)
                normalise(n_sb, z_sb, half, s_norm)

            def bc(small):
                return small.unsqueeze(2).to_broadcast([P, HG, EXPERTS])

            def best(half, k, logits):
                link(nc.vector.tensor_reduce(top[:, half, k], logits, AX, ALU.max))
                link(nc.vector.tensor_tensor(t8[:], logits, bc(top[:, half, k]), ALU.is_equal))
                link(nc.vector.tensor_tensor(t8[:], t8[:], pick[:].unsqueeze(1).to_broadcast([P, HG, EXPERTS]), ALU.mult))
                link(nc.vector.tensor_reduce(tmax[:], t8[:], AX, ALU.max))
                link(nc.vector.tensor_tensor(oh[:, half, k], t8[:], bc(tmax[:]), ALU.is_equal))

            for half in range(HALVES):
                dve.wait_ge(s_lg, half + 1)
                link(nc.vector.tensor_tensor(lg[:], bank[5 + half][:, 0:HG * EXPERTS].rearrange("p (g e) -> p g e", e=EXPERTS),
                                             br_sb[:].unsqueeze(1).to_broadcast([P, HG, EXPERTS]), ALU.add))
                best(half, 0, lg[:])
                link(nc.vector.scalar_tensor_tensor(lg2[:, half], oh[:, half, 0], -3e38, lg[:], ALU.mult, ALU.add))
                best(half, 1, lg2[:, half])
                nc.vector.tensor_tensor(gd[:, half], top[:, half, 1], top[:, half, 0], ALU.subtract).then_inc(s_gdiff, 1)
            for half in range(HALVES):
                dve.wait_ge(s_gexp, half + 1)
                link(nc.vector.tensor_scalar(tmax[:], gate[:, half, 1], 1.0, None, ALU.add))
                link(nc.vector.reciprocal(gate[:, half, 0], tmax[:]))
                link(nc.vector.tensor_tensor(gate[:, half, 1], gate[:, half, 1], gate[:, half, 0], ALU.mult))
                link(nc.vector.tensor_tensor(t8[:], oh[:, half, 0], bc(gate[:, half, 0]), ALU.mult))
                link(nc.vector.tensor_tensor(oh[:, half, 1], oh[:, half, 1], bc(gate[:, half, 1]), ALU.mult))
                nc.vector.tensor_tensor(G[:, half], t8[:], oh[:, half, 1], ALU.add).then_inc(s_G, 1)
            for half in range(HALVES):
                hs = slice(half * HG, (half + 1) * HG)
                dve.wait_ge(s_hz, half + 1)
                dve.wait_ge(s_b2y, half + 1)
                nc.vector.tensor_tensor(acc[:, hs], bank[5 + half][:].rearrange("p (g d) -> p g d", d=D), acc[:, hs],
                                        ALU.add).then_inc(s_acc, 1)
            for n in range(HALVES * EXPERTS):
                half, e = divmod(n, EXPERTS)
                dve.wait_ge(s_y, n + 1)
                dve.wait_ge(s_acc, HALVES + n)
                for j in range(HG):
                    g = half * HG + j
                    last = nc.vector.scalar_tensor_tensor(acc[:, g], bank[OUT_BANKS[n % 2]][:, j * D:(j + 1) * D],
                                                          G[:, half, j, e:e + 1], acc[:, g], ALU.mult, ALU.add)
                last.then_inc(s_acc, 1)


def kernel(**inputs):
    import numpy as np
    import concourse.bacc as bacc
    from concourse.bass_utils import run_bass_kernel_spmd

    a = {k: np.asarray(v) for k, v in inputs.items()}
    n_side = IMG // PATCH
    x = a["x"].reshape(BATCH, CHANNELS, n_side, PATCH, n_side, PATCH).transpose(1, 3, 5, 0, 2, 4)
    x = x.reshape(KC, P, GROUPS, P).transpose(1, 2, 0, 3)
    arrays = {
        "x_t": x,
        "w_tok": a["L0_tok_W"].T.reshape(KC, P, D).transpose(1, 0, 2),
        "w_attn": np.stack([a["L0_attn_" + n] for n in ("Wq", "Wk", "Wv", "Wo")]).transpose(1, 0, 2),
        "rows": np.broadcast_to(np.stack([a["L0_tok_b"], a["L0_attn_bv"], a["L0_attn_bo"]]), (P, 3, D)),
        "cols": np.stack([a[n] for n in ("L0_attn_bq", "L0_attn_bk", "L0_ffn_ln_g", "L0_ffn_ln_b")], axis=1),
        "w_router": a["L0_ffn_w_r"].T,
        "b_router": np.broadcast_to(a["L0_ffn_b_r"], (P, EXPERTS)),
        "w1": a["L0_ffn_W1"].transpose(1, 0, 2),
        "b1": a["L0_ffn_b1"].reshape(EXPERTS * FC, P).T,
        "w2": a["L0_ffn_W2"].reshape(EXPERTS, FC, P, D).transpose(2, 0, 1, 3),
        "b2": a["L0_ffn_b2"],
    }
    arrays = {k: np.ascontiguousarray(v) for k, v in arrays.items()}
    nc = bacc.Bacc("TRN2", target_bir_lowering=False, num_devices=1)
    args = [nc.dram_tensor(f"in_{k}", v.shape, mybir.dt.from_np(v.dtype), kind="ExternalInput").ap()
            for k, v in arrays.items()]
    out = nc.dram_tensor("out_tokens", (P, GROUPS, D), mybir.dt.float32, kind="ExternalOutput").ap()
    vit_tower(nc, *args, out)
    r = run_bass_kernel_spmd(nc, [{f"in_{k}": v for k, v in arrays.items()}], core_ids=[0])
    return r.results[0]["out_tokens"].transpose(1, 0, 2).reshape(BATCH, SEQ, D)
```

```python
from contextlib import ExitStack

import concourse.bass as bass
from concourse import mybir

BATCH, CHANNELS, IMG, PATCH, D = 64, 3, 64, 16, 128
SEQ = (IMG // PATCH) ** 2
TOKENS = BATCH * SEQ
PATCH_DIM = CHANNELS * PATCH * PATCH
HEADS = 8
DH = D // HEADS
EXPERTS, HID = 8, 512
EPS = 1e-5
SCALE = 1.0 / float(D) ** 0.5

P = 128
KC = PATCH_DIM // P
FC = HID // P
GROUPS = TOKENS // P
HALVES = 2
HG = GROUPS // HALVES
HT = TOKENS // HALVES
IPG = P // SEQ
HI = BATCH // HALVES
QKV_BANKS = ((3, 4, 5), (6, 7, 0))
SLOT_BANKS = (5, 6)
HID_BANKS = (7, 1)
OUT_BANKS = (3, 4)

TILES = (2 * HT - EXPERTS) // P + EXPERTS
TILE_SHIFT = P.bit_length() - 1
ROUND = 3
ROUNDS = TILES // ROUND
assert ROUNDS * ROUND == TILES
MAX_TILES = HT // P
W2_AT, B1_AT = HID, 2 * HID
BUNDLE = B1_AT + FC
RING = 2 * ROUND
BIAS_BANKS = (0, 2)
Q_SHARE = 5
P_SHARE = (5, 0)
CONSTS = 10
ROUTE_BANKS = (7, 2)
NMIN = 96


def vit_tower(nc, x_t, w_tok, w_attn, rows, cols, w_router, b_router, w1, b1, w2, b2, sorted_x, slot_ids, pair_y, out):
    fp32, bf16, i32 = mybir.dt.float32, mybir.dt.bfloat16, mybir.dt.int32
    ALU = mybir.AluOpType
    ACT = mybir.ActivationFunctionType
    AX = mybir.AxisListType.X

    with ExitStack() as ctx:
        def sb(name, shape, dt=fp32):
            return ctx.enter_context(nc.sbuf_tensor(name, shape, dt))

        def sem(name):
            return ctx.enter_context(nc.semaphore(name))

        x_sb = sb("x_sb", [P, GROUPS * KC * P])
        patches_sb = x_sb[:].rearrange("p (g c t) -> p g c t", c=KC, t=P)
        slots_sb = x_sb[:, 0:HALVES * TILES * D].rearrange("p (n t d) -> p n t d", n=HALVES, d=D)
        wtok_sb = sb("wtok_sb", [P, KC, D])
        wqkvo = sb("wqkvo", [P, 4, D])
        rows_sb = sb("rows_sb", [P, 3, D])
        cols_sb = sb("cols_sb", [P, 4])
        wr_sb = sb("wr_sb", [P, EXPERTS])
        br_sb = sb("br_sb", [P, EXPERTS])
        experts = sb("experts", [P, EXPERTS * BUNDLE])
        bundle = experts[:].rearrange("p (e w) -> p e w", w=BUNDLE)
        b2_blk = sb("b2_blk", [HG * EXPERTS, HG, D])
        ident = sb("ident", [P, P])
        mask16 = sb("mask16", [P, IPG])
        pick = sb("pick", [P, EXPERTS])
        below = sb("below", [P, P], bf16)
        ones = sb("ones", [P, P], bf16)
        full = sb("full", [P, MAX_TILES])
        tile_no = sb("tile_no", [P, TILES])
        ones8 = sb("ones8", [P, EXPERTS])
        zeros = sb("zeros", [P, D])
        h_sb = sb("h_sb", [P, GROUPS, D])
        hbo_sb = sb("hbo_sb", [P, GROUPS, D])
        z_sb = sb("z_sb", [P, GROUPS, D])
        n_sb = sb("n_sb", [P, GROUPS, D])
        acc = hbo_sb
        y_t = sb("y_t", [P, HALVES, HT])
        q_t = sb("q_t", [P, HALVES, HT])
        k_t = sb("k_t", [P, HALVES, HT])
        spread = sb("spread", [P, HALVES, HI * HEADS * SEQ])
        q_bd = spread[:].rearrange("p n (i h s) -> p n i h s", h=HEADS, s=SEQ)
        p_bd = spread[:].rearrange("p n (g h i s) -> p n g h i s", h=HEADS, i=IPG, s=SEQ)
        v_sb = sb("v_sb", [P, HALVES * HG * HEADS * D])
        v_pad = v_sb[:].rearrange("p (n g h d) -> p n g h d", g=HG, h=HEADS, d=D)
        y_rows = v_sb[:, 0:HALVES * TILES * D]
        y_sb = y_rows.rearrange("p (n t d) -> p n t d", t=TILES, d=D)
        back = v_sb[:, HALVES * TILES * D:HALVES * (TILES + 2 * HG) * D].rearrange(
            "p (n k g d) -> p n k g d", k=2, g=HG, d=D)
        e_sb = sb("e_sb", [P, HALVES, HI, SEQ])
        pt_sb = sb("pt_sb", [P, HALVES, HG * HEADS, SEQ])
        att_t = q_t
        hh_t = y_t
        slots_t = sb("slots_t", [P, 2, ROUND * P])
        hid = sb("hid", [P, 2, FC, P])
        wbuf = sb("wbuf", [P, RING, BUNDLE])
        st6 = sb("st6", [P, HG, 6])
        mv = sb("mv", [P, HG, 2])
        var = sb("var", [P, 2, HG])
        work = sb("work", [P, 2, HG])
        rstd = sb("rstd", [P, 2, HG])
        mx = sb("mx", [P, HALVES, HI])
        sm = sb("sm", [P, HALVES, HI])
        rs = sb("rs", [P, HALVES, HI])
        lg = sb("lg", [P, HG, EXPERTS])
        t8 = sb("t8", [P, HG, EXPERTS])
        oh = sb("oh", [P, HALVES, 2, HG, EXPERTS])
        top = sb("top", [P, HALVES, 2, HG])
        tmax = sb("tmax", [P, HG])
        gd = sb("gd", [P, HALVES, HG])
        th = sb("th", [P, HALVES, HG])
        gate = sb("gate", [P, HALVES, 2, HG])
        lg2 = sb("lg2", [P, HALVES, HG, EXPERTS])
        G = sb("G", [P, HALVES, HG, EXPERTS])
        g_t = sb("g_t", [HG * EXPERTS, HALVES, P])
        pick2 = sb("pick2", [P, HG, EXPERTS])
        before = sb("before", [P, HALVES, HG + 1, EXPERTS])
        before_bf = sb("before_bf", [P, HALVES, EXPERTS], bf16)
        more = sb("more", [P, EXPERTS, MAX_TILES])
        ntile = sb("ntile", [P, EXPERTS])
        tile_end = sb("tile_end", [P, EXPERTS])
        slot0 = sb("slot0", [P, EXPERTS])
        slot = sb("slot", [P, HG, EXPERTS])
        chosen = sb("chosen", [P, 2, HG, EXPERTS])
        dest_f = sb("dest_f", [P, 2, HG])
        dest = sb("dest", [P, HALVES, 2, HG], i32)
        ended = sb("ended", [P, TILES, EXPERTS])
        tile_f = sb("tile_f", [P, TILES])
        pair_id = sb("pair_id", [P, 2, HG], i32)
        spare_id = sb("spare_id", [P, TILES], i32)
        slot_tile = sb("slot_tile", [P, 2, HG], i32)
        slot_row = sb("slot_row", [P, 2, HG], i32)
        id_at = sb("id_at", [P, HALVES, 2, HG], i32)
        ids = sb("ids", [P, HALVES, TILES], i32)
        tile_expert = sb("tile_expert", [P, HALVES, TILES], i32)

        bank = [ctx.enter_context(nc.psum_tensor(f"bank{i}", [P, HT], fp32)) for i in range(8)]

        def spread_out(half, i):
            return p_bd[:, half, :, :, i].rearrange("p g h s -> p (g h) s")

        def v_diagonal(half, j):
            rows_ = v_pad[:, half, j].rearrange("p h d -> p (h d)")
            return bass.AP(tensor=rows_.tensor, offset=rows_.offset, ap=[rows_.ap[0], [D + DH, HEADS], [1, DH]])

        s_x = [sem(f"s_x{g}") for g in range(GROUPS)]
        s_w = [sem(f"s_w{e}") for e in range(EXPERTS)]
        (s_wtok, s_wattn, s_rows, s_cols, s_router) = (
            sem(n) for n in ("s_wtok", "s_wattn", "s_rows", "s_cols", "s_router"))
        (s_const, s_pool, s_vzero, s_dve) = (sem(n) for n in ("s_const", "s_pool", "s_vzero", "s_dve"))
        (s_patch, s_h, s_hbo, s_norm, s_tr, s_yt) = (
            sem(n) for n in ("s_patch", "s_h", "s_hbo", "s_norm", "s_tr", "s_yt"))
        (s_qkv, s_qt, s_kt, s_vp, s_qbd, s_qbda, s_sc, s_sub, s_exp, s_p) = (
            sem(n) for n in ("s_qkv", "s_qt", "s_kt", "s_vp", "s_qbd", "s_qbda", "s_sc", "s_sub", "s_exp", "s_p"))
        (s_pT, s_ptc, s_pbd, s_pbda, s_pv, s_at, s_o, s_z) = (
            sem(n) for n in ("s_pT", "s_ptc", "s_pbd", "s_pbda", "s_pv", "s_at", "s_o", "s_z"))
        (s_hht, s_lg, s_gdiff, s_th, s_counts, s_rank, s_dest, s_id_at, s_texp, s_hz) = (
            sem(n) for n in ("s_hht", "s_lg", "s_gdiff", "s_th", "s_counts", "s_rank", "s_dest", "s_id_at", "s_texp", "s_hz"))
        s_clear = [sem(f"s_clear{n}") for n in range(HALVES)]
        s_spare = [sem(f"s_spare{n}") for n in range(HALVES)]
        s_scatter = [sem(f"s_scatter{n}") for n in range(HALVES)]
        s_slots = [[sem(f"s_slots{n}_{k}") for k in range(2)] for n in range(HALVES)]
        s_id_scatter = [sem(f"s_id_scatter{n}") for n in range(HALVES)]
        s_ids = [sem(f"s_ids{n}") for n in range(HALVES)]
        s_pairs = [sem(f"s_pairs{n}") for n in range(HALVES)]
        s_back = [[sem(f"s_back{n}_{j}") for j in range(HG)] for n in range(HALVES)]
        (s_st, s_slt, s_wcopy, s_hid, s_gelu, s_y, s_yo, s_acc, s_out) = (
            sem(n) for n in ("s_st", "s_slt", "s_wcopy", "s_hid", "s_gelu", "s_y", "s_yo", "s_acc", "s_out"))

        (s_b2zero, s_b2, s_G, s_gT, s_gtc, s_b2y, s_accb) = (
            sem(n) for n in ("s_b2zero", "s_b2", "s_G", "s_gT", "s_gtc", "s_b2y", "s_accb"))

        tile_row = tile_expert[0:1].rearrange("p n t -> p (n t)")

        block = ctx.enter_context(nc.Block())

        @block.sync
        def _(sp):
            sp.dma_start(wtok_sb[:], w_tok).then_inc(s_wtok, 16)
            for g in range(GROUPS):
                sp.dma_start(patches_sb[:, g], x_t[:, g]).then_inc(s_x[g], 16)
                if g == HG - 1:
                    sp.dma_start(wqkvo[:], w_attn).then_inc(s_wattn, 16)
            sp.wait_ge(s_vzero, 3)
            for half in range(HALVES):
                sp.dma_start(sorted_x[half].rearrange("(t p) d -> p t d", p=P),
                             zeros[:].unsqueeze(1).to_broadcast([P, TILES, D])).then_inc(s_clear[half], 16)
            sp.wait_ge(s_const, CONSTS)
            for half in range(HALVES):
                sp.dma_start(slot_ids[half].rearrange("(p t) o -> p (t o)", p=P), spare_id[:]).then_inc(s_spare[half], 16)
            sp.wait_ge(s_b2zero, 1)
            for j in range(HG):
                sp.dma_start(b2_blk[j * EXPERTS:(j + 1) * EXPERTS, j], b2).then_inc(s_b2, 16)
            for e in range(EXPERTS):
                sp.dma_start(bundle[:, e, 0:HID], w1[:, e]).then_inc(s_w[e], 16)
                sp.dma_start(bundle[:, e, W2_AT:W2_AT + HID], w2[:, e]).then_inc(s_w[e], 16)
                sp.dma_start(bundle[:, e, B1_AT:B1_AT + FC], b1[:, e]).then_inc(s_w[e], 16)

            def load_slots(half):
                sp.wait_ge(s_scatter[half], 16 * 2 * HG)
                tiles = sorted_x[half].rearrange("(t p) d -> p t d", p=P)
                sp.dma_start(slots_sb[:, half, 0:ROUND], tiles[:, 0:ROUND]).then_inc(s_slots[half][0], 16)
                sp.dma_start(slots_sb[:, half, ROUND:TILES], tiles[:, ROUND:TILES]).then_inc(s_slots[half][1], 16)

            def load_ids(half):
                sp.wait_ge(s_id_scatter[half], 16 * 2 * HG)
                sp.dma_start(ids[:, half], slot_ids[half].rearrange("(p t) o -> p (t o)", p=P)).then_inc(s_ids[half], 16)

            def load_pairs(half):
                sp.wait_ge(s_pairs[half], 16 * TILES)
                rows_ = pair_y[half][0:2 * HT].rearrange("(k g p) d -> p k g d", k=2, p=P)
                for j in range(HG):
                    sp.dma_start(back[:, half, :, j], rows_[:, :, j]).then_inc(s_back[half][j], 16)

            for half in range(HALVES):
                load_slots(half)
                load_ids(half)
            for half in range(HALVES):
                load_pairs(half)
            for half in range(HALVES):
                for j in range(HG):
                    g = half * HG + j
                    sp.wait_ge(s_acc, 2 * (g + 1))
                    sp.dma_start(out[:, g], acc[:, g]).then_inc(s_out, 16)
            sp.wait_ge(s_out, 16 * GROUPS)

        @block.gpsimd
        def _(pool):
            nc.gpsimd.memset(ident[:], 0.0).then_inc(s_pool, 1)
            nc.gpsimd.memset(mask16[:], 1.0).then_inc(s_pool, 1)
            nc.gpsimd.memset(ones[:], 1.0).then_inc(s_pool, 1)
            nc.gpsimd.memset(ones8[:], 1.0).then_inc(s_const, 1)
            nc.gpsimd.memset(before[:, :, 0], 0.0).then_inc(s_const, 1)
            nc.gpsimd.iota(pick[:], pattern=[[-1, EXPERTS]], base=EXPERTS, channel_multiplier=0,
                           allow_small_or_imprecise_dtypes=True).then_inc(s_const, 1)
            nc.gpsimd.iota(full[:], pattern=[[P, MAX_TILES]], base=0, channel_multiplier=0,
                           allow_small_or_imprecise_dtypes=True).then_inc(s_const, 1)
            nc.gpsimd.iota(tile_no[:], pattern=[[1, TILES]], base=0, channel_multiplier=0,
                           allow_small_or_imprecise_dtypes=True).then_inc(s_const, 1)
            nc.gpsimd.iota(pair_id[:], pattern=[[HT, 2], [P, HG]], base=0, channel_multiplier=1).then_inc(s_const, 1)
            nc.gpsimd.iota(spare_id[:], pattern=[[P, TILES]], base=2 * HT, channel_multiplier=1).then_inc(s_const, 1)
            pool.wait_ge(s_pool, 3)
            nc.gpsimd.affine_select(out=ident[:], in_=ident[:], compare_op=ALU.not_equal, fill=1.0, base=0,
                                    pattern=[[-1, P]], channel_multiplier=1).then_inc(s_const, 1)
            nc.gpsimd.affine_select(out=below[:], in_=ones[:], compare_op=ALU.is_gt, fill=0.0, base=0,
                                    pattern=[[1, P]], channel_multiplier=-1).then_inc(s_const, 1)
            nc.gpsimd.affine_select(out=mask16[:], in_=mask16[:], compare_op=ALU.is_ge, fill=0.0, base=0,
                                    pattern=[[-SEQ, IPG]], channel_multiplier=1).then_inc(s_pool, 1)
            pool.wait_ge(s_pool, 4)
            nc.gpsimd.affine_select(out=mask16[:], in_=mask16[:], compare_op=ALU.is_ge, fill=0.0, base=SEQ - 1,
                                    pattern=[[SEQ, IPG]], channel_multiplier=-1).then_inc(s_const, 1)
            nc.gpsimd.memset(b2_blk[:], 0.0).then_inc(s_b2zero, 1)
            nc.gpsimd.memset(v_pad[:, 1], 0.0).then_inc(s_vzero, 1)

            pool.wait_ge(s_rows, 16)
            for half in range(HALVES):
                pool.wait_ge(s_h, half + 1)
                hs = slice(half * HG, (half + 1) * HG)
                nc.gpsimd.tensor_tensor(hbo_sb[:, hs], h_sb[:, hs], rows_sb[:, 2:3].to_broadcast([P, HG, D]),
                                        ALU.add).then_inc(s_hbo, 1)
            def scatter(half):
                pool.wait_ge(s_dest, half + 1)
                pool.wait_ge(s_clear[half], 16)
                for k in range(2):
                    for j in range(HG):
                        pool.indirect_dma_start(
                            out=sorted_x[half], out_offset=bass.IndirectOffsetOnAxis(ap=dest[:, half, k, j:j + 1], axis=0),
                            in_=n_sb[:, half * HG + j], in_offset=None).then_inc(s_scatter[half], 16)

            def base(half):
                pool.wait_ge(s_z, half + 1)
                hs = slice(half * HG, (half + 1) * HG)
                nc.gpsimd.tensor_tensor(acc[:, hs], h_sb[:, hs], z_sb[:, hs], ALU.add).then_inc(s_hz, 1)

            def scatter_ids(half):
                pool.wait_ge(s_id_at, half + 1)
                pool.wait_ge(s_spare[half], 16)
                for k in range(2):
                    for j in range(HG):
                        pool.indirect_dma_start(
                            out=slot_ids[half], out_offset=bass.IndirectOffsetOnAxis(ap=id_at[:, half, k, j:j + 1], axis=0),
                            in_=pair_id[:, k, j:j + 1], in_offset=None).then_inc(s_id_scatter[half], 16)

            scatter(0)
            base(0)
            scatter_ids(0)
            scatter(1)
            scatter_ids(1)
            base(1)
            for half in range(HALVES):
                pool.wait_ge(s_ids[half], 16)
                for t in range(TILES):
                    pool.wait_ge(s_yo, half * TILES + t + 1)
                    pool.indirect_dma_start(
                        out=pair_y[half], out_offset=bass.IndirectOffsetOnAxis(ap=ids[:, half, t:t + 1], axis=0),
                        in_=y_sb[:, half, t], in_offset=None).then_inc(s_pairs[half], 16)

        @block.tensor
        def _(pe):
            def patches(half):
                for j in range(HG):
                    g = half * HG + j
                    pe.wait_ge(s_x[g], 16)
                    for c in range(KC):
                        last = nc.tensor.matmul(bank[half][:, j * D:(j + 1) * D], patches_sb[:, g, c], wtok_sb[:, c],
                                                start=(c == 0), stop=(c == KC - 1))
                    last.then_inc(s_patch, 1)

            def transposes(to, src, done):
                for j in range(HG):
                    last = nc.tensor.transpose(to[:, j * P:(j + 1) * P], src(j), ident[:])
                last.then_inc(done, 1)

            def qkv(half):
                q_bank, k_bank, v_bank = QKV_BANKS[half]
                pe.wait_ge(s_yt, half + 1)
                nc.tensor.matmul(bank[q_bank][:], wqkvo[:, 0], y_t[:, half], start=True, stop=True).then_inc(s_qkv, 1)
                nc.tensor.matmul(bank[k_bank][:], wqkvo[:, 1], y_t[:, half], start=True, stop=True).then_inc(s_qkv, 1)
                for j in range(HG):
                    last = nc.tensor.matmul(bank[v_bank][:, j * D:(j + 1) * D], y_t[:, half, j * P:(j + 1) * P],
                                            wqkvo[:, 2], start=True, stop=True)
                last.then_inc(s_qkv, 1)

            def scores(half):
                pe.wait_ge(s_qbd, Q_SHARE * (half + 1))
                pe.wait_ge(s_qbda, (HEADS - Q_SHARE) * (half + 1))
                pe.wait_ge(s_kt, half + 1)
                for i in range(HI):
                    at = i * SEQ
                    n = NMIN if at + NMIN <= HT else SEQ
                    last = nc.tensor.matmul(bank[1 + half][:, at:at + n], q_bd[:, half, i].rearrange("p h s -> p (h s)"),
                                            k_t[:, half, at:at + n], start=True, stop=True)
                last.then_inc(s_sc, 1)

            def weighted(half):
                pe.wait_ge(s_pbd, sum(P_SHARE[:half + 1]))
                pe.wait_ge(s_pbda, IPG * (half + 1) - sum(P_SHARE[:half + 1]))
                pe.wait_ge(s_vp, half + 1)
                for j in range(HG):
                    for hd in range(HEADS):
                        last = nc.tensor.matmul(bank[5 + half][:, j * P:(j + 1) * P], v_pad[:, half, j, hd],
                                                p_bd[:, half, j, hd].rearrange("p i s -> p (i s)"),
                                                start=(hd == 0), stop=(hd == HEADS - 1))
                last.then_inc(s_pv, 1)

            def project(half):
                pe.wait_ge(s_at, half + 1)
                for j in range(HG):
                    last = nc.tensor.matmul(bank[(7, 0)[half]][:, j * D:(j + 1) * D], att_t[:, half, j * P:(j + 1) * P],
                                            wqkvo[:, 3], start=True, stop=True)
                last.then_inc(s_o, 1)

            def router_rows(half):
                pe.wait_ge(s_norm, HALVES + half + 1)
                transposes(bank[1 + half], rows_of(half), s_tr)

            def router(half):
                pe.wait_ge(s_hht, half + 1)
                for j in range(HG):
                    last = nc.tensor.matmul(bank[ROUTE_BANKS[half]][:, j * EXPERTS:(j + 1) * EXPERTS],
                                            hh_t[:, half, j * P:(j + 1) * P], wr_sb[:], start=True, stop=True)
                last.then_inc(s_lg, 1)

            def rank(half):
                pe.wait_ge(s_counts, half + 1)
                to = bank[ROUTE_BANKS[half]]
                nc.tensor.matmul(to[:, 0:EXPERTS], below[:], before_bf[:, half], start=True, stop=True)
                nc.tensor.matmul(to[:, EXPERTS:2 * EXPERTS], ones[:], before_bf[:, half],
                                 start=True, stop=True).then_inc(s_rank, 1)

            def transpose_gates():
                for half in range(HALVES):
                    pe.wait_ge(s_G, half + 1)
                    nc.tensor.transpose(bank[BIAS_BANKS[half]][0:HG * EXPERTS, 0:P],
                                        G[:, half].rearrange("p g e -> p (g e)"), ident[:]).then_inc(s_gT, 1)

            def bias2():
                pe.wait_ge(s_b2, 16 * HG)
                for half in range(HALVES):
                    pe.wait_ge(s_gtc, half + 1)
                    nc.tensor.matmul(bank[BIAS_BANKS[half]][:], g_t[:, half], b2_blk[:].rearrange("p g d -> p (g d)"),
                                     start=True, stop=True).then_inc(s_b2y, 1)

            def slots(r):
                half, q = divmod(r, ROUNDS)
                pe.wait_ge(s_slots[half][min(q, 1)], 16)
                if r >= 2:
                    pe.wait_ge(s_slt, r - 1)
                for j in range(ROUND):
                    last = nc.tensor.transpose(bank[SLOT_BANKS[r % 2]][:, j * P:(j + 1) * P],
                                               slots_sb[:, half, q * ROUND + j], ident[:])
                last.then_inc(s_st, 1)

            def up(n):
                r, b = divmod(n, ROUND)
                if b == 0:
                    pe.wait_ge(s_slt, r + 1)
                pe.wait_ge(s_wcopy, n + 1)
                if n >= 2:
                    pe.wait_ge(s_gelu, FC * (n - 1))
                for c in range(FC):
                    last = nc.tensor.matmul(bank[HID_BANKS[n % 2]][:, c * P:(c + 1) * P], wbuf[:, n % RING, c * P:(c + 1) * P],
                                            slots_t[:, r % 2, b * P:(b + 1) * P], start=True, stop=True)
                last.then_inc(s_hid, 1)

            def down(n):
                pe.wait_ge(s_gelu, FC * (n + 1))
                if n >= 2:
                    pe.wait_ge(s_yo, n - 1)
                for c in range(FC):
                    last = nc.tensor.matmul(bank[OUT_BANKS[n % 2]][:, 0:D], hid[:, n % 2, c],
                                            wbuf[:, n % RING, W2_AT + c * D:W2_AT + (c + 1) * D],
                                            start=(c == 0), stop=(c == FC - 1))
                last.then_inc(s_y, 1)

            def rows_of(half):
                return lambda j: n_sb[:, half * HG + j]

            def weights_of(half):
                return lambda j: e_sb[:, half, j * IPG:(j + 1) * IPG].rearrange("p i s -> p (i s)")

            pe.wait_ge(s_wtok, 16)
            patches(0)
            patches(1)
            pe.wait_ge(s_const, CONSTS)
            pe.wait_ge(s_wattn, 16)
            pe.wait_ge(s_norm, 1)
            transposes(bank[2], rows_of(0), s_tr)
            qkv(0)
            pe.wait_ge(s_norm, 2)
            pe.wait_ge(s_yt, 1)
            transposes(bank[2], rows_of(1), s_tr)
            scores(0)
            qkv(1)
            pe.wait_ge(s_p, 1)
            transposes(bank[3], weights_of(0), s_pT)
            weighted(0)
            pe.wait_ge(s_kt, HALVES)
            project(0)
            scores(1)
            pe.wait_ge(s_router, 32)
            router_rows(0)
            router(0)
            pe.wait_ge(s_p, 2)
            transposes(bank[4], weights_of(1), s_pT)
            rank(0)
            weighted(1)
            project(1)
            slots(0)
            up(0)
            for n in range(1, HALVES * TILES):
                if n % ROUND == ROUND - 1 and n + 1 < HALVES * TILES:
                    slots(n // ROUND + 1)
                up(n)
                down(n - 1)
                if n == ROUND - 1:
                    router_rows(1)
                if n == ROUND:
                    router(1)
                if n == 2 * ROUND - 1:
                    rank(1)
                if n == 4 * ROUND - 1:
                    transpose_gates()
                if n == 5 * ROUND - 1:
                    bias2()
            down(HALVES * TILES - 1)

        @block.scalar
        def _(act):
            act.dma_start(rows_sb[:], rows).then_inc(s_rows, 16)
            act.dma_start(cols_sb[:], cols).then_inc(s_cols, 16)
            act.dma_start(wr_sb[:], w_router).then_inc(s_router, 16)
            act.dma_start(br_sb[:], b_router).then_inc(s_router, 16)
            act.wait_ge(s_cols, 16)
            act.wait_ge(s_const, CONSTS)
            def rows_transposed(half):
                act.wait_ge(s_tr, half + 1)
                nc.scalar.activation(y_t[:, half], bank[2][:], ACT.Identity).then_inc(s_yt, 1)

            def project_q(half):
                act.wait_ge(s_qkv, 3 * half + 1)
                nc.scalar.activation(q_t[:, half], bank[QKV_BANKS[half][0]][:], ACT.Identity,
                                     bias=cols_sb[:, 0:1]).then_inc(s_qt, 1)

            def project_k(half):
                act.wait_ge(s_qkv, 3 * half + 2)
                nc.scalar.activation(k_t[:, half], bank[QKV_BANKS[half][1]][:], ACT.Identity,
                                     bias=cols_sb[:, 1:2]).then_inc(s_kt, 1)

            def spread_q(half):
                act.wait_ge(s_qt, half + 1)
                for hd in range(Q_SHARE, HEADS):
                    nc.scalar.activation(q_bd[:, half, :, hd], q_t[:, half].rearrange("p (i s) -> p i s", s=SEQ),
                                         ACT.Copy, scale=mask16[:, hd:hd + 1]).then_inc(s_qbda, 1)

            def exponentials(half):
                act.wait_ge(s_sub, half + 1)
                nc.scalar.activation(e_sb[:, half], e_sb[:, half], ACT.Exp, scale=SCALE).then_inc(s_exp, 1)

            def spread_weights(half):
                if P_SHARE[half] == 0:
                    act.wait_ge(s_pT, half + 1)
                    nc.scalar.activation(pt_sb[:, half].rearrange("p a b -> p (a b)"), bank[3 + half][:],
                                         ACT.Identity).then_inc(s_ptc, 1)
                act.wait_ge(s_ptc, half + 1)
                for i in range(P_SHARE[half], IPG):
                    nc.scalar.activation(spread_out(half, i), pt_sb[:, half], ACT.Copy,
                                         scale=mask16[:, i:i + 1]).then_inc(s_pbda, 1)

            def attended(half):
                act.wait_ge(s_pv, half + 1)
                nc.scalar.activation(att_t[:, half], bank[5 + half][:], ACT.Identity).then_inc(s_at, 1)

            def to_router(half):
                act.wait_ge(s_tr, HALVES + half + 1)
                nc.scalar.activation(hh_t[:, half], bank[1 + half][:], ACT.Identity, scale=cols_sb[:, 2:3],
                                     bias=cols_sb[:, 3:4]).then_inc(s_hht, 1)

            def gate_tanh(half):
                act.wait_ge(s_gdiff, half + 1)
                nc.scalar.activation(th[:, half], gd[:, half], ACT.Tanh, scale=0.5).then_inc(s_th, 1)

            def copy_output(n, par):
                act.wait_ge(s_y, n + 1)
                nc.scalar.activation(y_rows[:, bass.ds(n * D, D)], bank[OUT_BANKS[par]][:, 0:D],
                                     ACT.Copy).then_inc(s_yo, 1)

            def expert_round(r, buf, first=False):
                for b in range(ROUND):
                    n = r * ROUND + b
                    par = (buf * ROUND + b) % 2
                    act.wait_ge(s_hid, n + 1)
                    for c in range(FC):
                        nc.scalar.activation(hid[:, par, c], bank[HID_BANKS[par]][:, c * P:(c + 1) * P],
                                             ACT.Gelu, bias=wbuf[:, buf * ROUND + b, B1_AT + c:B1_AT + c + 1]).then_inc(s_gelu, 1)
                    if not (first and b == 0):
                        copy_output(n - 1, 1 - par)

            rows_transposed(0)
            project_q(0)
            project_k(0)
            spread_q(0)
            rows_transposed(1)
            project_q(1)
            exponentials(0)
            project_k(1)
            spread_weights(0)
            spread_q(1)
            attended(0)
            to_router(0)
            exponentials(1)
            spread_weights(1)
            attended(1)
            expert_round(0, 0, first=True)
            to_router(1)
            expert_round(1, 1)
            expert_round(2, 0)
            gate_tanh(0)
            gate_tanh(1)
            expert_round(3, 1)
            for half in range(HALVES):
                act.wait_ge(s_gT, half + 1)
                nc.scalar.activation(g_t[:, half], bank[BIAS_BANKS[half]][0:HG * EXPERTS, 0:P],
                                     ACT.Copy).then_inc(s_gtc, 1)
            with act.Fori(2, ROUNDS) as pair:
                expert_round(2 * pair, 0)
                expert_round(2 * pair + 1, 1)
            copy_output(HALVES * TILES - 1, 1)

        @block.vector
        def _(dve):
            chain = [0]

            def link(ins):
                chain[0] += 1
                ins.then_inc(s_dve, 1)
                dve.wait_ge(s_dve, chain[0])

            def moments(src, half):
                for j in range(HG):
                    last = nc.vector.bn_stats(st6[:, j], src[:, half * HG + j])
                link(last)
                for j in range(HG):
                    last = nc.vector.bn_aggr(mv[:, j], st6[:, j])
                link(last)

            def inverse_root(v, w, y):
                link(nc.vector.tensor_scalar(y.bitcast(i32), v.bitcast(i32), -0.5, float(0x5F3759DF), ALU.mult, ALU.add))
                link(nc.vector.tensor_tensor(w, y, y, ALU.mult))
                link(nc.vector.tensor_tensor(w, w, v, ALU.mult))
                link(nc.vector.scalar_tensor_tensor(w, w, -10 / 3, w, ALU.add, ALU.mult))
                link(nc.vector.scalar_tensor_tensor(y, w, 5.0, y, ALU.add, ALU.mult))
                link(nc.vector.tensor_tensor(w, y, y, ALU.mult))
                link(nc.vector.scalar_tensor_tensor(w, w, -0.5 * 0.375 ** 3, v, ALU.mult, ALU.mult))
                link(nc.vector.scalar_tensor_tensor(y, w, 1.5 * 0.375, y, ALU.add, ALU.mult))

            def normalise(dst, src, half, scale, done):
                for j in range(HG):
                    g = half * HG + j
                    last = nc.vector.tensor_scalar(dst[:, g], src[:, g], mv[:, j, 0:1], scale[:, j:j + 1],
                                                   ALU.subtract, ALU.mult)
                last.then_inc(done, 1)

            def spread_q(half):
                dve.wait_ge(s_qt, half + 1)
                for hd in range(Q_SHARE):
                    nc.vector.tensor_scalar(q_bd[:, half, :, hd], q_t[:, half].rearrange("p (i s) -> p i s", s=SEQ),
                                            mask16[:, hd:hd + 1], None, ALU.mult).then_inc(s_qbd, 1)

            def spread_v(half):
                dve.wait_ge(s_qkv, 3 * half + 3)
                for j in range(HG):
                    nc_last = nc.vector.tensor_tensor(
                        v_diagonal(half, j), bank[QKV_BANKS[half][2]][:, j * D:(j + 1) * D].rearrange("p (h d) -> p h d", d=DH),
                        rows_sb[:, 1].rearrange("p (h d) -> p h d", d=DH), ALU.add)
                nc_last.then_inc(s_vp, 1)

            nc.vector.memset(zeros[:], 0.0).then_inc(s_vzero, 1)
            nc.vector.memset(v_pad[:, 0], 0.0).then_inc(s_vzero, 1)
            dve.wait_ge(s_rows, 16)
            for half in range(HALVES):
                hs = slice(half * HG, (half + 1) * HG)
                dve.wait_ge(s_patch, HG * (half + 1))
                nc.vector.tensor_tensor(h_sb[:, hs], bank[half][:].rearrange("p (g d) -> p g d", d=D),
                                        rows_sb[:, 0:1].to_broadcast([P, HG, D]), ALU.add).then_inc(s_h, 1)
                dve.wait_ge(s_h, half + 1)
                moments(h_sb, half)
                link(nc.vector.tensor_scalar(var[:, 0], mv[:, :, 1], EPS, None, ALU.add))
                inverse_root(var[:, 0], work[:, 0], rstd[:, 0])
                normalise(n_sb, h_sb, half, rstd[:, 0], s_norm)
            dve.wait_ge(s_const, CONSTS)
            dve.wait_ge(s_vzero, 3)

            def below_maximum(half):
                sc = bank[1 + half][:].rearrange("p (i s) -> p i s", s=SEQ)
                dve.wait_ge(s_sc, half + 1)
                link(nc.vector.tensor_reduce(mx[:, half], sc, AX, ALU.max))
                nc.vector.tensor_tensor(e_sb[:, half], sc, mx[:, half].unsqueeze(2).to_broadcast([P, HI, SEQ]),
                                        ALU.subtract).then_inc(s_sub, 1)

            def over_sum(half):
                dve.wait_ge(s_exp, half + 1)
                link(nc.vector.tensor_reduce(sm[:, half], e_sb[:, half], AX, ALU.add))
                link(nc.vector.reciprocal(rs[:, half], sm[:, half]))
                nc.vector.tensor_tensor(e_sb[:, half], e_sb[:, half], rs[:, half].unsqueeze(2).to_broadcast([P, HI, SEQ]),
                                        ALU.mult).then_inc(s_p, 1)

            def spread_weights(half):
                dve.wait_ge(s_pT, half + 1)
                nc.vector.tensor_copy(pt_sb[:, half].rearrange("p a b -> p (a b)"), bank[3 + half][:]).then_inc(s_ptc, 1)
                dve.wait_ge(s_ptc, half + 1)
                for i in range(P_SHARE[half]):
                    nc.vector.tensor_scalar(spread_out(half, i), pt_sb[:, half], mask16[:, i:i + 1], None,
                                            ALU.mult).then_inc(s_pbd, 1)

            def residual(half):
                hs = slice(half * HG, (half + 1) * HG)
                dve.wait_ge(s_hbo, half + 1)
                dve.wait_ge(s_o, half + 1)
                link(nc.vector.tensor_tensor(h_sb[:, hs], bank[(7, 0)[half]][:].rearrange("p (g d) -> p g d", d=D),
                                             hbo_sb[:, hs], ALU.add))
                moments(h_sb, half)

            def normalised_rows(half):
                link(nc.vector.tensor_scalar(var[:, 0], mv[:, :, 1], EPS, None, ALU.add))
                link(nc.vector.scalar_tensor_tensor(var[:, 1], var[:, 0], EPS, mv[:, :, 1], ALU.mult, ALU.add))
                inverse_root(var[:], work[:], rstd[:])
                dve.wait_ge(s_tr, half + 1)
                normalise(n_sb, h_sb, half, rstd[:, 1], s_norm)
                normalise(z_sb, h_sb, half, rstd[:, 0], s_z)

            def bc(small):
                return small.unsqueeze(2).to_broadcast([P, HG, EXPERTS])

            def best(half, k, logits):
                link(nc.vector.tensor_reduce(top[:, half, k], logits, AX, ALU.max))
                link(nc.vector.tensor_tensor(t8[:], logits, bc(top[:, half, k]), ALU.is_equal))
                link(nc.vector.tensor_tensor(pick2[:], t8[:], pick[:].unsqueeze(1).to_broadcast([P, HG, EXPERTS]), ALU.mult))
                link(nc.vector.tensor_reduce(tmax[:], pick2[:], AX, ALU.max))
                link(nc.vector.tensor_tensor(oh[:, half, k], pick2[:], bc(tmax[:]), ALU.is_equal))

            def choose(half):
                dve.wait_ge(s_lg, half + 1)
                link(nc.vector.tensor_tensor(
                    lg[:], bank[ROUTE_BANKS[half]][:, 0:HG * EXPERTS].rearrange("p (g e) -> p g e", e=EXPERTS),
                    br_sb[:].unsqueeze(1).to_broadcast([P, HG, EXPERTS]), ALU.add))
                best(half, 0, lg[:])
                link(nc.vector.scalar_tensor_tensor(lg2[:, half], oh[:, half, 0], -3e38, lg[:], ALU.mult, ALU.add))
                best(half, 1, lg2[:, half])
                nc.vector.tensor_tensor(gd[:, half], top[:, half, 1], top[:, half, 0], ALU.subtract).then_inc(s_gdiff, 1)
                link(nc.vector.tensor_tensor(t8[:], oh[:, half, 0], oh[:, half, 1], ALU.add))
                for j in range(HG):
                    link(nc.vector.tensor_tensor(before[:, half, j + 1], before[:, half, j], t8[:, j], ALU.add))
                nc.vector.tensor_copy(before_bf[:, half], before[:, half, HG]).then_inc(s_counts, 1)

            def place(half):
                dve.wait_ge(s_rank, half + 1)
                count = bank[ROUTE_BANKS[half]][:, EXPERTS:2 * EXPERTS]
                rank_ = bank[ROUTE_BANKS[half]][:, 0:EXPERTS]
                link(nc.vector.tensor_tensor(more[:], count.unsqueeze(2).to_broadcast([P, EXPERTS, MAX_TILES]),
                                             full[:].unsqueeze(1).to_broadcast([P, EXPERTS, MAX_TILES]), ALU.is_gt))
                link(nc.vector.tensor_reduce(ntile[:], more[:], AX, ALU.add))
                link(nc.vector.tensor_tensor_scan(tile_end[:], ones8[:], ntile[:], 0.0, ALU.mult, ALU.add))
                link(nc.vector.tensor_tensor(slot0[:], tile_end[:], ntile[:], ALU.subtract))
                link(nc.vector.scalar_tensor_tensor(slot0[:], slot0[:], float(P), rank_, ALU.mult, ALU.add))
                link(nc.vector.tensor_tensor(slot[:], before[:, half, 0:HG],
                                             slot0[:].unsqueeze(1).to_broadcast([P, HG, EXPERTS]), ALU.add))
                for k in range(2):
                    link(nc.vector.tensor_tensor(chosen[:, k], slot[:], oh[:, half, k], ALU.mult))
                link(nc.vector.tensor_reduce(dest_f[:], chosen[:], AX, ALU.add))
                nc.vector.tensor_copy(dest[:, half], dest_f[:]).then_inc(s_dest, 1)
                link(nc.vector.tensor_tensor(ended[:], tile_no[:].unsqueeze(2).to_broadcast([P, TILES, EXPERTS]),
                                             tile_end[:].unsqueeze(1).to_broadcast([P, TILES, EXPERTS]), ALU.is_ge))
                link(nc.vector.tensor_reduce(tile_f[:], ended[:], AX, ALU.add))
                nc.vector.tensor_scalar(tile_expert[:, half], tile_f[:], float(EXPERTS - 1), None,
                                        ALU.min).then_inc(s_texp, 1)
                dve.wait_ge(s_dest, half + 1)
                nc.vector.tensor_scalar(slot_tile[:], dest[:, half], TILE_SHIFT, None, ALU.arith_shift_right)
                link(nc.vector.tensor_scalar(slot_row[:], dest[:, half], P - 1, None, ALU.bitwise_and))
                nc.vector.scalar_tensor_tensor(id_at[:, half], slot_row[:], float(TILES), slot_tile[:],
                                               ALU.mult, ALU.add).then_inc(s_id_at, 1)

            def gates(half):
                dve.wait_ge(s_th, half + 1)
                for k in range(2):
                    link(nc.vector.tensor_scalar(gate[:, half, k], th[:, half], (-0.5, 0.5)[k], 0.5, ALU.mult, ALU.add))
                for k in range(2):
                    link(nc.vector.tensor_tensor(chosen[:, k], oh[:, half, k], bc(gate[:, half, k]), ALU.mult))
                nc.vector.tensor_tensor(G[:, half], chosen[:, 0], chosen[:, 1], ALU.add).then_inc(s_G, 1)

            def fetch(n, b, first=False):
                if not first:
                    dve.wait_ge(s_y, n - RING + 1)
                e = dve.value_load(tile_row[:, bass.ds(n, 1)], min_val=0, max_val=EXPERTS - 1)
                nc.vector.tensor_copy(wbuf[:, b], experts[:, bass.ds(e * BUNDLE, BUNDLE)]).then_inc(s_wcopy, 1)

            def transposed(r, buf):
                dve.wait_ge(s_st, r + 1)
                nc.vector.tensor_scalar(slots_t[:, buf], bank[SLOT_BANKS[buf]][:, 0:ROUND * P], cols_sb[:, 2:3],
                                        cols_sb[:, 3:4], ALU.mult, ALU.add).then_inc(s_slt, 1)

            def expert_round(r, buf):
                transposed(r, buf)
                for b in range(ROUND):
                    fetch((r + 1) * ROUND + b, (1 - buf) * ROUND + b)

            def add_bias(half):
                hs = slice(half * HG, (half + 1) * HG)
                dve.wait_ge(s_hz, half + 1)
                dve.wait_ge(s_b2y, half + 1)
                nc.vector.tensor_tensor(acc[:, hs], bank[BIAS_BANKS[half]][:].rearrange("p (g d) -> p g d", d=D),
                                        acc[:, hs], ALU.add).then_inc(s_accb, 1)

            def combine(half):
                dve.wait_ge(s_accb, half + 1)
                for j in range(HG):
                    g = half * HG + j
                    dve.wait_ge(s_back[half][j], 16)
                    for k in range(2):
                        nc.vector.scalar_tensor_tensor(acc[:, g], back[:, half, k, j], gate[:, half, k, j:j + 1],
                                                       acc[:, g], ALU.mult, ALU.add).then_inc(s_acc, 1)
                        dve.wait_ge(s_acc, 2 * g + k + 1)

            spread_q(0)
            spread_v(0)
            below_maximum(0)
            over_sum(0)
            spread_weights(0)
            spread_q(1)
            spread_v(1)
            residual(0)
            normalised_rows(0)
            below_maximum(1)
            over_sum(1)
            choose(0)
            place(0)
            for e in range(EXPERTS):
                dve.wait_ge(s_w[e], 48)
            dve.wait_ge(s_texp, 1)
            for n in range(RING):
                fetch(n, n, first=True)
            dve.wait_ge(s_cols, 16)
            transposed(0, 0)
            residual(1)
            normalised_rows(1)
            transposed(1, 1)
            for b in range(ROUND):
                fetch(RING + b, b)
            choose(1)
            transposed(2, 0)
            place(1)
            dve.wait_ge(s_texp, 2)
            for b in range(ROUND):
                fetch(RING + ROUND + b, ROUND + b)
            expert_round(3, 1)
            gates(0)
            gates(1)
            with dve.Fori(2, ROUNDS - 1) as pair:
                expert_round(2 * pair, 0)
                expert_round(2 * pair + 1, 1)
            expert_round(2 * ROUNDS - 2, 0)
            transposed(2 * ROUNDS - 1, 1)
            add_bias(0)
            add_bias(1)
            combine(0)
            combine(1)


def kernel(**inputs):
    import numpy as np
    import concourse.bacc as bacc
    from concourse.bass_utils import run_bass_kernel_spmd

    a = {k: np.asarray(v) for k, v in inputs.items()}
    n_side = IMG // PATCH
    x = a["x"].reshape(BATCH, CHANNELS, n_side, PATCH, n_side, PATCH).transpose(1, 3, 5, 0, 2, 4)
    x = x.reshape(KC, P, GROUPS, P).transpose(1, 2, 0, 3)
    arrays = {
        "x_t": x,
        "w_tok": a["L0_tok_W"].T.reshape(KC, P, D).transpose(1, 0, 2),
        "w_attn": np.stack([a["L0_attn_" + n] for n in ("Wq", "Wk", "Wv", "Wo")]).transpose(1, 0, 2),
        "rows": np.broadcast_to(np.stack([a["L0_tok_b"], a["L0_attn_bv"], a["L0_attn_bo"]]), (P, 3, D)),
        "cols": np.stack([a[n] for n in ("L0_attn_bq", "L0_attn_bk", "L0_ffn_ln_g", "L0_ffn_ln_b")], axis=1),
        "w_router": a["L0_ffn_w_r"].T,
        "b_router": np.broadcast_to(a["L0_ffn_b_r"], (P, EXPERTS)),
        "w1": a["L0_ffn_W1"].transpose(1, 0, 2),
        "b1": a["L0_ffn_b1"].reshape(EXPERTS, FC, P).transpose(2, 0, 1),
        "w2": a["L0_ffn_W2"].reshape(EXPERTS, FC, P, D).transpose(2, 0, 1, 3),
        "b2": a["L0_ffn_b2"],
    }
    arrays = {k: np.ascontiguousarray(v) for k, v in arrays.items()}
    nc = bacc.Bacc("TRN2", target_bir_lowering=False, num_devices=1)
    args = [nc.dram_tensor(f"in_{k}", v.shape, mybir.dt.from_np(v.dtype), kind="ExternalInput").ap()
            for k, v in arrays.items()]
    args += [[nc.dram_tensor(f"{name}{half}", shape, dt, kind="Internal").ap() for half in range(HALVES)]
             for name, shape, dt in (("sorted_x", (TILES * P, D), mybir.dt.float32),
                                     ("slot_ids", (TILES * P, 1), mybir.dt.int32),
                                     ("pair_y", (2 * HT + TILES * P, D), mybir.dt.float32))]
    out = nc.dram_tensor("out_tokens", (P, GROUPS, D), mybir.dt.float32, kind="ExternalOutput").ap()
    vit_tower(nc, *args, out)
    r = run_bass_kernel_spmd(nc, [{f"in_{k}": v for k, v in arrays.items()}], core_ids=[0])
    return r.results[0]["out_tokens"].transpose(1, 0, 2).reshape(BATCH, SEQ, D)
```

```python
from contextlib import ExitStack

import concourse.bass as bass
from concourse import mybir

BATCH, CHANNELS, IMG, PATCH, D = 64, 3, 64, 16, 128
SEQ = (IMG // PATCH) ** 2
TOKENS = BATCH * SEQ
PATCH_DIM = CHANNELS * PATCH * PATCH
HEADS = 8
DH = D // HEADS
EXPERTS, HID = 8, 512
EPS = 1e-5
SCALE = 1.0 / float(D) ** 0.5

P = 128
KC = PATCH_DIM // P
FC = HID // P
GROUPS = TOKENS // P
HALVES = 2
HG = GROUPS // HALVES
HT = TOKENS // HALVES
IPG = P // SEQ
HI = BATCH // HALVES
QKV_BANKS = ((3, 4, 5), (6, 7, 0))
SLOT_BANKS = (5, 6)
HID_BANKS = (7, 1)
OUT_BANKS = (3, 4)

TILES = (2 * HT - EXPERTS) // P + EXPERTS
TILE_SHIFT = P.bit_length() - 1
ROUND = 3
ROUNDS = TILES // ROUND
assert ROUNDS * ROUND == TILES
MAX_TILES = HT // P
W2_AT, B1_AT = HID, 2 * HID
BUNDLE = B1_AT + FC
RING = 2 * ROUND
BIAS_BANKS = (0, 2)
Q_SHARE = 5
P_SHARE = (5, 0)
CONSTS = 10
ROUTE_BANKS = (7, 2)
NMIN = 96


def vit_tower(nc, x_t, w_tok, w_attn, rows, cols, w_router, b_router, w1, b1, w2, b2, sorted_x, slot_ids, pair_y, out):
    fp32, bf16, i32 = mybir.dt.float32, mybir.dt.bfloat16, mybir.dt.int32
    ALU = mybir.AluOpType
    ACT = mybir.ActivationFunctionType
    AX = mybir.AxisListType.X

    with ExitStack() as ctx:
        def sb(name, shape, dt=fp32):
            return ctx.enter_context(nc.sbuf_tensor(name, shape, dt))

        def sem(name):
            return ctx.enter_context(nc.semaphore(name))

        x_sb = sb("x_sb", [P, GROUPS * KC * P])
        patches_sb = x_sb[:].rearrange("p (g c t) -> p g c t", c=KC, t=P)
        slots_sb = x_sb[:, 0:HALVES * TILES * D].rearrange("p (n t d) -> p n t d", n=HALVES, d=D)
        wtok_sb = sb("wtok_sb", [P, KC, D])
        wqkvo = sb("wqkvo", [P, 4, D])
        rows_sb = sb("rows_sb", [P, 3, D])
        cols_sb = sb("cols_sb", [P, 4])
        wr_sb = sb("wr_sb", [P, EXPERTS])
        br_sb = sb("br_sb", [P, EXPERTS])
        experts = sb("experts", [P, EXPERTS * BUNDLE])
        bundle = experts[:].rearrange("p (e w) -> p e w", w=BUNDLE)
        b2_blk = sb("b2_blk", [HG * EXPERTS, HG, D])
        ident = sb("ident", [P, P])
        mask16 = sb("mask16", [P, IPG])
        expert_no = sb("expert_no", [P, EXPERTS])
        below = sb("below", [P, P], bf16)
        ones = sb("ones", [P, P], bf16)
        full = sb("full", [P, MAX_TILES])
        tile_no = sb("tile_no", [P, TILES])
        ones8 = sb("ones8", [P, EXPERTS])
        zeros = sb("zeros", [P, D])
        warm = sb("warm", [P, 1])
        h_sb = sb("h_sb", [P, GROUPS, D])
        hbo_sb = sb("hbo_sb", [P, GROUPS, D])
        z_sb = sb("z_sb", [P, GROUPS, D])
        n_sb = sb("n_sb", [P, GROUPS, D])
        acc = hbo_sb
        y_t = sb("y_t", [P, HALVES, HT])
        q_t = sb("q_t", [P, HALVES, HT])
        k_t = sb("k_t", [P, HALVES, HT])
        spread = sb("spread", [P, HALVES, HI * HEADS * SEQ])
        q_bd = spread[:].rearrange("p n (i h s) -> p n i h s", h=HEADS, s=SEQ)
        p_bd = spread[:].rearrange("p n (g h i s) -> p n g h i s", h=HEADS, i=IPG, s=SEQ)
        v_sb = sb("v_sb", [P, HALVES * HG * HEADS * D])
        v_pad = v_sb[:].rearrange("p (n g h d) -> p n g h d", g=HG, h=HEADS, d=D)
        y_rows = v_sb[:, 0:HALVES * TILES * D]
        y_sb = y_rows.rearrange("p (n t d) -> p n t d", t=TILES, d=D)
        back = v_sb[:, HALVES * TILES * D:HALVES * (TILES + 2 * HG) * D].rearrange(
            "p (n k g d) -> p n k g d", k=2, g=HG, d=D)
        e_sb = sb("e_sb", [P, HALVES, HI, SEQ])
        pt_sb = sb("pt_sb", [P, HALVES, HG * HEADS, SEQ])
        att_t = q_t
        hh_t = y_t
        slots_t = sb("slots_t", [P, 2, ROUND * P])
        hid = sb("hid", [P, 2, FC, P])
        wbuf = sb("wbuf", [P, RING, BUNDLE])
        st6 = sb("st6", [P, HG, 6])
        mv = sb("mv", [P, HG, 2])
        var = sb("var", [P, 2, HG])
        work = sb("work", [P, 2, HG])
        rstd = sb("rstd", [P, 2, HG])
        mx = sb("mx", [P, HALVES, HI])
        sm = sb("sm", [P, HALVES, HI])
        rs = sb("rs", [P, HALVES, HI])
        lg = sb("lg", [P, HG, EXPERTS])
        oh = sb("oh", [P, HALVES, 2, HG, EXPERTS])
        sorted_lg = sb("sorted_lg", [P, HG, EXPERTS])
        sorted_e = sb("sorted_e", [P, HG, EXPERTS], mybir.dt.uint32)
        gd = sb("gd", [P, HALVES, HG])
        th = sb("th", [P, HALVES, HG])
        gate = sb("gate", [P, HALVES, 2, HG])
        G = sb("G", [P, HALVES, HG, EXPERTS])
        g_t = sb("g_t", [HG * EXPERTS, HALVES, P])
        both = sb("both", [P, HALVES, HG + 1, EXPERTS], bf16)
        more = sb("more", [P, EXPERTS, MAX_TILES])
        ntile = sb("ntile", [P, EXPERTS])
        tile_end = sb("tile_end", [P, EXPERTS])
        slot0 = sb("slot0", [P, EXPERTS])
        slot = sb("slot", [P, HG, EXPERTS])
        chosen = sb("chosen", [P, 2, HG, EXPERTS])
        dest_f = sb("dest_f", [P, 2, HG])
        dest = sb("dest", [P, HALVES, 2, HG], i32)
        ended = sb("ended", [P, TILES, EXPERTS])
        tile_f = sb("tile_f", [P, TILES])
        pair_id = sb("pair_id", [P, 2, HG], i32)
        spare_id = sb("spare_id", [P, TILES], i32)
        slot_tile = sb("slot_tile", [P, 2, HG], i32)
        slot_row = sb("slot_row", [P, 2, HG], i32)
        id_at = sb("id_at", [P, HALVES, 2, HG], i32)
        ids = sb("ids", [P, HALVES, TILES], i32)
        tile_expert = sb("tile_expert", [P, HALVES, TILES], i32)

        bank = [ctx.enter_context(nc.psum_tensor(f"bank{i}", [P, HT], fp32)) for i in range(8)]

        def spread_out(half, i):
            return p_bd[:, half, :, :, i].rearrange("p g h s -> p (g h) s")

        def v_diagonal(half, j):
            rows_ = v_pad[:, half, j].rearrange("p h d -> p (h d)")
            return bass.AP(tensor=rows_.tensor, offset=rows_.offset, ap=[rows_.ap[0], [D + DH, HEADS], [1, DH]])

        s_x = [sem(f"s_x{g}") for g in range(GROUPS)]
        s_w = [sem(f"s_w{e}") for e in range(EXPERTS)]
        s_x0b = sem("s_x0b")
        s_wtok = [sem(f"s_wtok{k}") for k in range(2)]
        (s_wattn, s_rows, s_cols, s_router) = (
            sem(n) for n in ("s_wattn", "s_rows", "s_cols", "s_router"))
        (s_const, s_pool, s_zeros, s_vzero, s_dve) = (sem(n) for n in ("s_const", "s_pool", "s_zeros", "s_vzero", "s_dve"))
        (s_patch, s_h, s_hbo, s_norm, s_tr, s_yt) = (
            sem(n) for n in ("s_patch", "s_h", "s_hbo", "s_norm", "s_tr", "s_yt"))
        (s_qkv, s_qt, s_kt, s_vp, s_qbd, s_qbda, s_sc, s_sub, s_exp, s_p) = (
            sem(n) for n in ("s_qkv", "s_qt", "s_kt", "s_vp", "s_qbd", "s_qbda", "s_sc", "s_sub", "s_exp", "s_p"))
        (s_pT, s_ptc, s_pbd, s_pbda, s_pv, s_at, s_o, s_z) = (
            sem(n) for n in ("s_pT", "s_ptc", "s_pbd", "s_pbda", "s_pv", "s_at", "s_o", "s_z"))
        (s_hht, s_lg, s_gdiff, s_th, s_counts, s_rank, s_dest, s_id_at, s_texp, s_hz) = (
            sem(n) for n in ("s_hht", "s_lg", "s_gdiff", "s_th", "s_counts", "s_rank", "s_dest", "s_id_at", "s_texp", "s_hz"))
        s_clear = [sem(f"s_clear{n}") for n in range(HALVES)]
        s_spare = [sem(f"s_spare{n}") for n in range(HALVES)]
        s_scatter = [sem(f"s_scatter{n}") for n in range(HALVES)]
        s_slots = [[sem(f"s_slots{n}_{k}") for k in range(2)] for n in range(HALVES)]
        s_id_scatter = [sem(f"s_id_scatter{n}") for n in range(HALVES)]
        s_ids = [sem(f"s_ids{n}") for n in range(HALVES)]
        s_pairs = [sem(f"s_pairs{n}") for n in range(HALVES)]
        s_back = [[sem(f"s_back{n}_{j}") for j in range(HG)] for n in range(HALVES)]
        (s_st, s_slt, s_wcopy, s_hid, s_gelu, s_y, s_yo, s_out) = (
            sem(n) for n in ("s_st", "s_slt", "s_wcopy", "s_hid", "s_gelu", "s_y", "s_yo", "s_out"))
        s_acc = [sem(f"s_acc{g}") for g in range(GROUPS)]

        (s_b2zero, s_b2, s_G, s_gT, s_gtc, s_b2y, s_accb) = (
            sem(n) for n in ("s_b2zero", "s_b2", "s_G", "s_gT", "s_gtc", "s_b2y", "s_accb"))

        tile_row = tile_expert[0:1].rearrange("p n t -> p (n t)")

        block = ctx.enter_context(nc.Block())

        @block.sync
        def _(sp):
            sp.dma_start(wtok_sb[:, 0:KC // 2], w_tok[:, 0:KC // 2]).then_inc(s_wtok[0], 16)
            sp.dma_start(patches_sb[:, 0, 0:KC // 2], x_t[:, 0, 0:KC // 2]).then_inc(s_x[0], 16)
            sp.dma_start(wtok_sb[:, KC // 2:KC], w_tok[:, KC // 2:KC]).then_inc(s_wtok[1], 16)
            sp.dma_start(patches_sb[:, 0, KC // 2:KC], x_t[:, 0, KC // 2:KC]).then_inc(s_x0b, 16)
            for g in range(1, GROUPS):
                sp.dma_start(patches_sb[:, g], x_t[:, g]).then_inc(s_x[g], 16)
                if g == HG - 1:
                    sp.dma_start(wqkvo[:], w_attn).then_inc(s_wattn, 16)
            sp.wait_ge(s_zeros, 1)
            for half in range(HALVES):
                sp.dma_start(sorted_x[half].rearrange("(t p) d -> p t d", p=P),
                             zeros[:].unsqueeze(1).to_broadcast([P, TILES, D])).then_inc(s_clear[half], 16)
            sp.wait_ge(s_const, CONSTS)
            for half in range(HALVES):
                sp.dma_start(slot_ids[half].rearrange("(p t) o -> p (t o)", p=P), spare_id[:]).then_inc(s_spare[half], 16)
            sp.wait_ge(s_b2zero, 1)
            for j in range(HG):
                sp.dma_start(b2_blk[j * EXPERTS:(j + 1) * EXPERTS, j], b2).then_inc(s_b2, 16)
            for e in range(EXPERTS):
                sp.dma_start(bundle[:, e, 0:HID], w1[:, e]).then_inc(s_w[e], 16)
                sp.dma_start(bundle[:, e, W2_AT:W2_AT + HID], w2[:, e]).then_inc(s_w[e], 16)
                sp.dma_start(bundle[:, e, B1_AT:B1_AT + FC], b1[:, e]).then_inc(s_w[e], 16)

            def load_slots(half):
                sp.wait_ge(s_scatter[half], 16 * 2 * HG)
                tiles = sorted_x[half].rearrange("(t p) d -> p t d", p=P)
                sp.dma_start(slots_sb[:, half, 0:ROUND], tiles[:, 0:ROUND]).then_inc(s_slots[half][0], 16)
                sp.dma_start(slots_sb[:, half, ROUND:TILES], tiles[:, ROUND:TILES]).then_inc(s_slots[half][1], 16)

            def load_ids(half):
                sp.wait_ge(s_id_scatter[half], 16 * 2 * HG)
                sp.dma_start(ids[:, half], slot_ids[half].rearrange("(p t) o -> p (t o)", p=P)).then_inc(s_ids[half], 16)

            def load_pairs(half):
                sp.wait_ge(s_pairs[half], 16 * TILES)
                rows_ = pair_y[half][0:2 * HT].rearrange("(k g p) d -> p k g d", k=2, p=P)
                for j in range(HG):
                    sp.dma_start(back[:, half, :, j], rows_[:, :, j]).then_inc(s_back[half][j], 16)

            for half in range(HALVES):
                load_slots(half)
                load_ids(half)
            for half in range(HALVES):
                load_pairs(half)
            for half in range(HALVES):
                for j in range(HG):
                    g = half * HG + j
                    sp.wait_ge(s_acc[g], 2)
                    sp.dma_start(out[:, g], acc[:, g]).then_inc(s_out, 16)
            sp.wait_ge(s_out, 16 * GROUPS)

        @block.gpsimd
        def _(pool):
            nc.gpsimd.memset(ident[:], 0.0).then_inc(s_pool, 1)
            nc.gpsimd.memset(mask16[:], 1.0).then_inc(s_pool, 1)
            nc.gpsimd.memset(ones[:], 1.0).then_inc(s_pool, 1)
            nc.gpsimd.memset(ones8[:], 1.0).then_inc(s_const, 1)
            nc.gpsimd.memset(both[:, :, HG], 0.0).then_inc(s_const, 1)
            nc.gpsimd.iota(expert_no[:], pattern=[[1, EXPERTS]], base=0, channel_multiplier=0,
                           allow_small_or_imprecise_dtypes=True).then_inc(s_const, 1)
            nc.gpsimd.iota(full[:], pattern=[[P, MAX_TILES]], base=0, channel_multiplier=0,
                           allow_small_or_imprecise_dtypes=True).then_inc(s_const, 1)
            nc.gpsimd.iota(tile_no[:], pattern=[[1, TILES]], base=0, channel_multiplier=0,
                           allow_small_or_imprecise_dtypes=True).then_inc(s_const, 1)
            nc.gpsimd.iota(pair_id[:], pattern=[[HT, 2], [P, HG]], base=0, channel_multiplier=1).then_inc(s_const, 1)
            nc.gpsimd.iota(spare_id[:], pattern=[[P, TILES]], base=2 * HT, channel_multiplier=1).then_inc(s_const, 1)
            pool.wait_ge(s_pool, 3)
            nc.gpsimd.affine_select(out=ident[:], in_=ident[:], compare_op=ALU.not_equal, fill=1.0, base=0,
                                    pattern=[[-1, P]], channel_multiplier=1).then_inc(s_const, 1)
            nc.gpsimd.affine_select(out=below[:], in_=ones[:], compare_op=ALU.is_gt, fill=0.0, base=0,
                                    pattern=[[1, P]], channel_multiplier=-1).then_inc(s_const, 1)
            nc.gpsimd.affine_select(out=mask16[:], in_=mask16[:], compare_op=ALU.is_ge, fill=0.0, base=0,
                                    pattern=[[-SEQ, IPG]], channel_multiplier=1).then_inc(s_pool, 1)
            pool.wait_ge(s_pool, 4)
            nc.gpsimd.affine_select(out=mask16[:], in_=mask16[:], compare_op=ALU.is_ge, fill=0.0, base=SEQ - 1,
                                    pattern=[[SEQ, IPG]], channel_multiplier=-1).then_inc(s_const, 1)
            nc.gpsimd.memset(b2_blk[:], 0.0).then_inc(s_b2zero, 1)
            nc.gpsimd.memset(v_pad[:, 1], 0.0).then_inc(s_vzero, 1)

            pool.wait_ge(s_rows, 16)
            for half in range(HALVES):
                pool.wait_ge(s_h, half + 1)
                hs = slice(half * HG, (half + 1) * HG)
                nc.gpsimd.tensor_tensor(hbo_sb[:, hs], h_sb[:, hs], rows_sb[:, 2:3].to_broadcast([P, HG, D]),
                                        ALU.add).then_inc(s_hbo, 1)

            def scatter(half):
                pool.wait_ge(s_dest, half + 1)
                pool.wait_ge(s_clear[half], 16)
                for k in range(2):
                    for j in range(HG):
                        pool.indirect_dma_start(
                            out=sorted_x[half], out_offset=bass.IndirectOffsetOnAxis(ap=dest[:, half, k, j:j + 1], axis=0),
                            in_=n_sb[:, half * HG + j], in_offset=None).then_inc(s_scatter[half], 16)

            def base(half):
                pool.wait_ge(s_z, half + 1)
                hs = slice(half * HG, (half + 1) * HG)
                nc.gpsimd.tensor_tensor(acc[:, hs], h_sb[:, hs], z_sb[:, hs], ALU.add).then_inc(s_hz, 1)

            def scatter_ids(half):
                pool.wait_ge(s_id_at, half + 1)
                pool.wait_ge(s_spare[half], 16)
                for k in range(2):
                    for j in range(HG):
                        pool.indirect_dma_start(
                            out=slot_ids[half], out_offset=bass.IndirectOffsetOnAxis(ap=id_at[:, half, k, j:j + 1], axis=0),
                            in_=pair_id[:, k, j:j + 1], in_offset=None).then_inc(s_id_scatter[half], 16)

            scatter(0)
            base(0)
            scatter_ids(0)
            scatter(1)
            scatter_ids(1)
            base(1)
            for half in range(HALVES):
                pool.wait_ge(s_ids[half], 16)
                for t in range(TILES):
                    pool.wait_ge(s_yo, half * TILES + t + 1)
                    pool.indirect_dma_start(
                        out=pair_y[half], out_offset=bass.IndirectOffsetOnAxis(ap=ids[:, half, t:t + 1], axis=0),
                        in_=y_sb[:, half, t], in_offset=None).then_inc(s_pairs[half], 16)

        @block.tensor
        def _(pe):
            def patches(half):
                for j in range(HG):
                    g = half * HG + j
                    pe.wait_ge(s_x[g], 16)
                    for c in range(KC):
                        if g == 0 and c % (KC // 2) == 0:
                            pe.wait_ge(s_wtok[2 * c // KC], 16)
                            if c:
                                pe.wait_ge(s_x0b, 16)
                        last = nc.tensor.matmul(bank[half][:, j * D:(j + 1) * D], patches_sb[:, g, c], wtok_sb[:, c],
                                                start=(c == 0), stop=(c == KC - 1))
                    last.then_inc(s_patch, 1)

            def transposes(to, src, done):
                for j in range(HG):
                    last = nc.tensor.transpose(to[:, j * P:(j + 1) * P], src(j), ident[:])
                last.then_inc(done, 1)

            def project_qk(half):
                pe.wait_ge(s_yt, half + 1)
                for w in range(2):
                    nc.tensor.matmul(bank[QKV_BANKS[half][w]][:], wqkvo[:, w], y_t[:, half],
                                     start=True, stop=True).then_inc(s_qkv, 1)

            def project_v(half):
                for j in range(HG):
                    last = nc.tensor.matmul(bank[QKV_BANKS[half][2]][:, j * D:(j + 1) * D],
                                            y_t[:, half, j * P:(j + 1) * P], wqkvo[:, 2], start=True, stop=True)
                last.then_inc(s_qkv, 1)

            def scores(half, images):
                pe.wait_ge(s_qbd, Q_SHARE * (half + 1))
                pe.wait_ge(s_qbda, (HEADS - Q_SHARE) * (half + 1))
                pe.wait_ge(s_kt, half + 1)
                for i in images:
                    at = i * SEQ
                    n = NMIN if at + NMIN <= HT else SEQ
                    last = nc.tensor.matmul(bank[1 + half][:, at:at + n], q_bd[:, half, i].rearrange("p h s -> p (h s)"),
                                            k_t[:, half, at:at + n], start=True, stop=True)
                if i == HI - 1:
                    last.then_inc(s_sc, 1)

            def weighted(half):
                pe.wait_ge(s_pbd, sum(P_SHARE[:half + 1]))
                pe.wait_ge(s_pbda, IPG * (half + 1) - sum(P_SHARE[:half + 1]))
                pe.wait_ge(s_vp, half + 1)
                for j in range(HG):
                    for hd in range(HEADS):
                        last = nc.tensor.matmul(bank[5 + half][:, j * P:(j + 1) * P], v_pad[:, half, j, hd],
                                                p_bd[:, half, j, hd].rearrange("p i s -> p (i s)"),
                                                start=(hd == 0), stop=(hd == HEADS - 1))
                last.then_inc(s_pv, 1)

            def project(half):
                pe.wait_ge(s_at, half + 1)
                for j in range(HG):
                    last = nc.tensor.matmul(bank[(7, 0)[half]][:, j * D:(j + 1) * D], att_t[:, half, j * P:(j + 1) * P],
                                            wqkvo[:, 3], start=True, stop=True)
                last.then_inc(s_o, 1)

            def router_rows(half):
                pe.wait_ge(s_norm, HALVES + half + 1)
                transposes(bank[1 + half], rows_of(half), s_tr)

            def router(half):
                pe.wait_ge(s_hht, half + 1)
                for j in range(HG):
                    last = nc.tensor.matmul(bank[ROUTE_BANKS[half]][:, j * EXPERTS:(j + 1) * EXPERTS],
                                            hh_t[:, half, j * P:(j + 1) * P], wr_sb[:], start=True, stop=True)
                last.then_inc(s_lg, 1)

            def rank(half):
                pe.wait_ge(s_counts, half + 1)
                to = bank[ROUTE_BANKS[half]][:, 0:(HG + 1) * EXPERTS].rearrange("p (g e) -> p g e", e=EXPERTS)
                nc.tensor.matmul(to, below[:], both[:, half], start=True, stop=False)
                for j in range(1, HG + 1):
                    last = nc.tensor.matmul(to[:, j:HG + 1], ones[:], both[:, half, 0:HG + 1 - j], start=False, stop=(j == HG))
                last.then_inc(s_rank, 1)

            def transpose_gates():
                for half in range(HALVES):
                    pe.wait_ge(s_G, half + 1)
                    nc.tensor.transpose(bank[BIAS_BANKS[half]][0:HG * EXPERTS, 0:P],
                                        G[:, half].rearrange("p g e -> p (g e)"), ident[:]).then_inc(s_gT, 1)

            def bias2():
                pe.wait_ge(s_b2, 16 * HG)
                for half in range(HALVES):
                    pe.wait_ge(s_gtc, half + 1)
                    nc.tensor.matmul(bank[BIAS_BANKS[half]][:], g_t[:, half], b2_blk[:].rearrange("p g d -> p (g d)"),
                                     start=True, stop=True).then_inc(s_b2y, 1)

            def slots(r):
                half, q = divmod(r, ROUNDS)
                pe.wait_ge(s_slots[half][min(q, 1)], 16)
                if r >= 2:
                    pe.wait_ge(s_slt, r - 1)
                for j in range(ROUND):
                    last = nc.tensor.transpose(bank[SLOT_BANKS[r % 2]][:, j * P:(j + 1) * P],
                                               slots_sb[:, half, q * ROUND + j], ident[:])
                last.then_inc(s_st, 1)

            def up(n):
                r, b = divmod(n, ROUND)
                if b == 0:
                    pe.wait_ge(s_slt, r + 1)
                pe.wait_ge(s_wcopy, n + 1)
                if n >= 2:
                    pe.wait_ge(s_gelu, FC * (n - 1))
                for c in range(FC):
                    last = nc.tensor.matmul(bank[HID_BANKS[n % 2]][:, c * P:(c + 1) * P], wbuf[:, n % RING, c * P:(c + 1) * P],
                                            slots_t[:, r % 2, b * P:(b + 1) * P], start=True, stop=True)
                last.then_inc(s_hid, 1)

            def down(n):
                pe.wait_ge(s_gelu, FC * (n + 1))
                if n >= 2:
                    pe.wait_ge(s_yo, n - 1)
                for c in range(FC):
                    last = nc.tensor.matmul(bank[OUT_BANKS[n % 2]][:, 0:D], hid[:, n % 2, c],
                                            wbuf[:, n % RING, W2_AT + c * D:W2_AT + (c + 1) * D],
                                            start=(c == 0), stop=(c == FC - 1))
                last.then_inc(s_y, 1)

            def rows_of(half):
                return lambda j: n_sb[:, half * HG + j]

            def weights_of(half):
                return lambda j: e_sb[:, half, j * IPG:(j + 1) * IPG].rearrange("p i s -> p (i s)")

            patches(0)
            patches(1)
            pe.wait_ge(s_const, CONSTS)
            pe.wait_ge(s_wattn, 16)
            pe.wait_ge(s_norm, 1)
            transposes(bank[2], rows_of(0), s_tr)
            project_qk(0)
            project_v(0)
            scores(0, range(0, HI // 2))
            pe.wait_ge(s_norm, 2)
            pe.wait_ge(s_yt, 1)
            transposes(bank[2], rows_of(1), s_tr)
            scores(0, range(HI // 2, HI))
            project_qk(1)
            pe.wait_ge(s_p, 1)
            transposes(bank[3], weights_of(0), s_pT)
            project_v(1)
            weighted(0)
            pe.wait_ge(s_kt, HALVES)
            project(0)
            scores(1, range(HI))
            pe.wait_ge(s_router, 32)
            router_rows(0)
            router(0)
            pe.wait_ge(s_p, 2)
            transposes(bank[4], weights_of(1), s_pT)
            rank(0)
            weighted(1)
            slots(0)
            project(1)
            up(0)
            for n in range(1, HALVES * TILES):
                if n % ROUND == ROUND - 1 and n + 1 < HALVES * TILES:
                    slots(n // ROUND + 1)
                up(n)
                down(n - 1)
                if n == ROUND - 1:
                    router_rows(1)
                if n == ROUND:
                    router(1)
                if n == 2 * ROUND - 1:
                    rank(1)
                if n == 4 * ROUND - 1:
                    transpose_gates()
                if n == 5 * ROUND - 1:
                    bias2()
            down(HALVES * TILES - 1)

        @block.scalar
        def _(act):
            act.dma_start(rows_sb[:], rows).then_inc(s_rows, 16)
            act.dma_start(cols_sb[:], cols).then_inc(s_cols, 16)
            act.dma_start(wr_sb[:], w_router).then_inc(s_router, 16)
            act.dma_start(br_sb[:], b_router).then_inc(s_router, 16)
            act.wait_ge(s_zeros, 1)
            nc.scalar.activation(warm[:], zeros[:, 0:1], ACT.Exp)
            act.wait_ge(s_cols, 16)
            act.wait_ge(s_const, CONSTS)

            def rows_transposed(half):
                act.wait_ge(s_tr, half + 1)
                nc.scalar.activation(y_t[:, half], bank[2][:], ACT.Identity).then_inc(s_yt, 1)

            def project_q(half):
                act.wait_ge(s_qkv, 3 * half + 1)
                nc.scalar.activation(q_t[:, half], bank[QKV_BANKS[half][0]][:], ACT.Identity,
                                     bias=cols_sb[:, 0:1]).then_inc(s_qt, 1)

            def project_k(half):
                act.wait_ge(s_qkv, 3 * half + 2)
                nc.scalar.activation(k_t[:, half], bank[QKV_BANKS[half][1]][:], ACT.Identity,
                                     bias=cols_sb[:, 1:2]).then_inc(s_kt, 1)

            def spread_q(half):
                act.wait_ge(s_qt, half + 1)
                for hd in range(Q_SHARE, HEADS):
                    nc.scalar.activation(q_bd[:, half, :, hd], q_t[:, half].rearrange("p (i s) -> p i s", s=SEQ),
                                         ACT.Copy, scale=mask16[:, hd:hd + 1]).then_inc(s_qbda, 1)

            def exponentials(half):
                act.wait_ge(s_sub, half + 1)
                nc.scalar.activation(e_sb[:, half], e_sb[:, half], ACT.Exp, scale=SCALE).then_inc(s_exp, 1)

            def spread_weights(half):
                if P_SHARE[half] == 0:
                    act.wait_ge(s_pT, half + 1)
                    nc.scalar.activation(pt_sb[:, half].rearrange("p a b -> p (a b)"), bank[3 + half][:],
                                         ACT.Identity).then_inc(s_ptc, 1)
                act.wait_ge(s_ptc, half + 1)
                for i in range(P_SHARE[half], IPG):
                    nc.scalar.activation(spread_out(half, i), pt_sb[:, half], ACT.Copy,
                                         scale=mask16[:, i:i + 1]).then_inc(s_pbda, 1)

            def attended(half):
                act.wait_ge(s_pv, half + 1)
                nc.scalar.activation(att_t[:, half], bank[5 + half][:], ACT.Identity).then_inc(s_at, 1)

            def to_router(half):
                act.wait_ge(s_tr, HALVES + half + 1)
                nc.scalar.activation(hh_t[:, half], bank[1 + half][:], ACT.Identity, scale=cols_sb[:, 2:3],
                                     bias=cols_sb[:, 3:4]).then_inc(s_hht, 1)

            def gate_tanh(half):
                act.wait_ge(s_gdiff, half + 1)
                nc.scalar.activation(th[:, half], gd[:, half], ACT.Tanh, scale=0.5).then_inc(s_th, 1)

            def copy_output(n, par):
                act.wait_ge(s_y, n + 1)
                nc.scalar.activation(y_rows[:, bass.ds(n * D, D)], bank[OUT_BANKS[par]][:, 0:D],
                                     ACT.Copy).then_inc(s_yo, 1)

            def expert_round(r, buf, first=False):
                for b in range(ROUND):
                    n = r * ROUND + b
                    par = (buf * ROUND + b) % 2
                    act.wait_ge(s_hid, n + 1)
                    for c in range(FC):
                        nc.scalar.activation(hid[:, par, c], bank[HID_BANKS[par]][:, c * P:(c + 1) * P],
                                             ACT.Gelu, bias=wbuf[:, buf * ROUND + b, B1_AT + c:B1_AT + c + 1]).then_inc(s_gelu, 1)
                    if not (first and b == 0):
                        copy_output(n - 1, 1 - par)

            rows_transposed(0)
            project_q(0)
            project_k(0)
            spread_q(0)
            rows_transposed(1)
            project_q(1)
            exponentials(0)
            project_k(1)
            spread_weights(0)
            spread_q(1)
            attended(0)
            to_router(0)
            exponentials(1)
            spread_weights(1)
            attended(1)
            expert_round(0, 0, first=True)
            to_router(1)
            expert_round(1, 1)
            expert_round(2, 0)
            gate_tanh(0)
            gate_tanh(1)
            expert_round(3, 1)
            for half in range(HALVES):
                act.wait_ge(s_gT, half + 1)
                nc.scalar.activation(g_t[:, half], bank[BIAS_BANKS[half]][0:HG * EXPERTS, 0:P],
                                     ACT.Copy).then_inc(s_gtc, 1)
            with act.Fori(2, ROUNDS) as pair:
                expert_round(2 * pair, 0)
                expert_round(2 * pair + 1, 1)
            copy_output(HALVES * TILES - 1, 1)

        @block.vector
        def _(dve):
            chain = [0]

            def link(ins):
                chain[0] += 1
                ins.then_inc(s_dve, 1)
                dve.wait_ge(s_dve, chain[0])

            def moments(src, half):
                for j in range(HG):
                    last = nc.vector.bn_stats(st6[:, j], src[:, half * HG + j])
                link(last)
                for j in range(HG):
                    last = nc.vector.bn_aggr(mv[:, j], st6[:, j])
                link(last)

            def inverse_root(v, w, y):
                link(nc.vector.tensor_scalar(y.bitcast(i32), v.bitcast(i32), -0.5, float(0x5F3759DF), ALU.mult, ALU.add))
                link(nc.vector.tensor_tensor(w, y, y, ALU.mult))
                link(nc.vector.tensor_tensor(w, w, v, ALU.mult))
                link(nc.vector.scalar_tensor_tensor(w, w, -10 / 3, w, ALU.add, ALU.mult))
                link(nc.vector.scalar_tensor_tensor(y, w, 5.0, y, ALU.add, ALU.mult))
                link(nc.vector.tensor_tensor(w, y, y, ALU.mult))
                link(nc.vector.scalar_tensor_tensor(w, w, -0.5 * 0.375 ** 3, v, ALU.mult, ALU.mult))
                link(nc.vector.scalar_tensor_tensor(y, w, 1.5 * 0.375, y, ALU.add, ALU.mult))

            def normalise(dst, src, half, scale, done):
                for j in range(HG):
                    g = half * HG + j
                    last = nc.vector.tensor_scalar(dst[:, g], src[:, g], mv[:, j, 0:1], scale[:, j:j + 1],
                                                   ALU.subtract, ALU.mult)
                last.then_inc(done, 1)

            def spread_q(half):
                dve.wait_ge(s_qt, half + 1)
                for hd in range(Q_SHARE):
                    nc.vector.tensor_scalar(q_bd[:, half, :, hd], q_t[:, half].rearrange("p (i s) -> p i s", s=SEQ),
                                            mask16[:, hd:hd + 1], None, ALU.mult).then_inc(s_qbd, 1)

            def spread_v(half):
                dve.wait_ge(s_qkv, 3 * half + 3)
                for j in range(HG):
                    last = nc.vector.tensor_tensor(
                        v_diagonal(half, j),
                        bank[QKV_BANKS[half][2]][:, j * D:(j + 1) * D].rearrange("p (h d) -> p h d", d=DH),
                        rows_sb[:, 1].rearrange("p (h d) -> p h d", d=DH), ALU.add)
                last.then_inc(s_vp, 1)

            nc.vector.memset(zeros[:], 0.0).then_inc(s_zeros, 1)
            nc.vector.memset(v_pad[:, 0], 0.0).then_inc(s_vzero, 1)
            dve.wait_ge(s_rows, 16)

            def embedded(half):
                hs = slice(half * HG, (half + 1) * HG)
                dve.wait_ge(s_patch, HG * (half + 1))
                nc.vector.tensor_tensor(h_sb[:, hs], bank[half][:].rearrange("p (g d) -> p g d", d=D),
                                        rows_sb[:, 0:1].to_broadcast([P, HG, D]), ALU.add).then_inc(s_h, 1)
                dve.wait_ge(s_h, half + 1)
                moments(h_sb, half)
                link(nc.vector.tensor_scalar(var[:, 0], mv[:, :, 1], EPS, None, ALU.add))
                inverse_root(var[:, 0], work[:, 0], rstd[:, 0])

            def below_maximum(half):
                sc = bank[1 + half][:].rearrange("p (i s) -> p i s", s=SEQ)
                dve.wait_ge(s_sc, half + 1)
                link(nc.vector.tensor_reduce(mx[:, half], sc, AX, ALU.max))
                nc.vector.tensor_tensor(e_sb[:, half], sc, mx[:, half].unsqueeze(2).to_broadcast([P, HI, SEQ]),
                                        ALU.subtract).then_inc(s_sub, 1)

            def over_sum(half):
                dve.wait_ge(s_exp, half + 1)
                link(nc.vector.tensor_reduce(sm[:, half], e_sb[:, half], AX, ALU.add))
                link(nc.vector.reciprocal(rs[:, half], sm[:, half]))
                nc.vector.tensor_tensor(e_sb[:, half], e_sb[:, half], rs[:, half].unsqueeze(2).to_broadcast([P, HI, SEQ]),
                                        ALU.mult).then_inc(s_p, 1)

            def spread_weights(half):
                dve.wait_ge(s_pT, half + 1)
                nc.vector.tensor_copy(pt_sb[:, half].rearrange("p a b -> p (a b)"), bank[3 + half][:]).then_inc(s_ptc, 1)
                dve.wait_ge(s_ptc, half + 1)
                for i in range(P_SHARE[half]):
                    nc.vector.tensor_scalar(spread_out(half, i), pt_sb[:, half], mask16[:, i:i + 1], None,
                                            ALU.mult).then_inc(s_pbd, 1)

            def residual(half):
                hs = slice(half * HG, (half + 1) * HG)
                dve.wait_ge(s_hbo, half + 1)
                dve.wait_ge(s_o, half + 1)
                link(nc.vector.tensor_tensor(h_sb[:, hs], bank[(7, 0)[half]][:].rearrange("p (g d) -> p g d", d=D),
                                             hbo_sb[:, hs], ALU.add))
                moments(h_sb, half)

            def twice_normalised(half):
                link(nc.vector.tensor_scalar(var[:, 0], mv[:, :, 1], EPS, None, ALU.add))
                link(nc.vector.scalar_tensor_tensor(var[:, 1], var[:, 0], EPS, mv[:, :, 1], ALU.mult, ALU.add))
                inverse_root(var[:], work[:], rstd[:])
                dve.wait_ge(s_tr, half + 1)
                normalise(n_sb, h_sb, half, rstd[:, 1], s_norm)

            def once_normalised(half):
                normalise(z_sb, h_sb, half, rstd[:, 0], s_z)

            def bc(small):
                return small.unsqueeze(2).to_broadcast([P, HG, EXPERTS])

            def choose(half):
                dve.wait_ge(s_lg, half + 1)
                link(nc.vector.tensor_tensor(
                    lg[:], bank[ROUTE_BANKS[half]][:, 0:HG * EXPERTS].rearrange("p (g e) -> p g e", e=EXPERTS),
                    br_sb[:].unsqueeze(1).to_broadcast([P, HG, EXPERTS]), ALU.add))
                for j in range(HG):
                    last = nc.vector.max(sorted_lg[:, j], lg[:, j])
                link(last)
                for j in range(HG):
                    last = nc.vector.max_index(sorted_e[:, j], sorted_lg[:, j], lg[:, j])
                link(last)
                nc.vector.tensor_tensor(gd[:, half], sorted_lg[:, :, 1], sorted_lg[:, :, 0], ALU.subtract).then_inc(s_gdiff, 1)
                for k in range(2):
                    last = nc.vector.tensor_tensor(oh[:, half, k], expert_no[:].unsqueeze(1).to_broadcast([P, HG, EXPERTS]),
                                                   bc(sorted_e[:, :, k]), ALU.is_equal)
                link(last)
                nc.vector.tensor_tensor(both[:, half, 0:HG], oh[:, half, 0], oh[:, half, 1], ALU.add).then_inc(s_counts, 1)

            def place(half):
                dve.wait_ge(s_rank, half + 1)
                before = bank[ROUTE_BANKS[half]][:, 0:(HG + 1) * EXPERTS].rearrange("p (g e) -> p g e", e=EXPERTS)
                count = before[:, HG]
                link(nc.vector.tensor_tensor(more[:], count.unsqueeze(2).to_broadcast([P, EXPERTS, MAX_TILES]),
                                             full[:].unsqueeze(1).to_broadcast([P, EXPERTS, MAX_TILES]), ALU.is_gt))
                link(nc.vector.tensor_reduce(ntile[:], more[:], AX, ALU.add))
                link(nc.vector.tensor_tensor_scan(tile_end[:], ones8[:], ntile[:], 0.0, ALU.mult, ALU.add))
                link(nc.vector.tensor_tensor(slot0[:], tile_end[:], ntile[:], ALU.subtract))
                link(nc.vector.scalar_tensor_tensor(slot[:], slot0[:].unsqueeze(1).to_broadcast([P, HG, EXPERTS]),
                                                    float(P), before[:, 0:HG], ALU.mult, ALU.add))
                for k in range(2):
                    link(nc.vector.tensor_tensor(chosen[:, k], slot[:], oh[:, half, k], ALU.mult))
                link(nc.vector.tensor_reduce(dest_f[:], chosen[:], AX, ALU.add))
                nc.vector.tensor_copy(dest[:, half], dest_f[:]).then_inc(s_dest, 1)
                link(nc.vector.tensor_tensor(ended[:], tile_no[:].unsqueeze(2).to_broadcast([P, TILES, EXPERTS]),
                                             tile_end[:].unsqueeze(1).to_broadcast([P, TILES, EXPERTS]), ALU.is_ge))
                link(nc.vector.tensor_reduce(tile_f[:], ended[:], AX, ALU.add))
                nc.vector.tensor_scalar(tile_expert[:, half], tile_f[:], float(EXPERTS - 1), None,
                                        ALU.min).then_inc(s_texp, 1)
                dve.wait_ge(s_dest, half + 1)
                nc.vector.tensor_scalar(slot_tile[:], dest[:, half], TILE_SHIFT, None, ALU.arith_shift_right)
                link(nc.vector.tensor_scalar(slot_row[:], dest[:, half], P - 1, None, ALU.bitwise_and))
                nc.vector.scalar_tensor_tensor(id_at[:, half], slot_row[:], float(TILES), slot_tile[:],
                                               ALU.mult, ALU.add).then_inc(s_id_at, 1)

            def gates(half):
                dve.wait_ge(s_th, half + 1)
                for k in range(2):
                    link(nc.vector.tensor_scalar(gate[:, half, k], th[:, half], (-0.5, 0.5)[k], 0.5, ALU.mult, ALU.add))
                for k in range(2):
                    link(nc.vector.tensor_tensor(chosen[:, k], oh[:, half, k], bc(gate[:, half, k]), ALU.mult))
                nc.vector.tensor_tensor(G[:, half], chosen[:, 0], chosen[:, 1], ALU.add).then_inc(s_G, 1)

            def fetch(n, b, first=False):
                if not first:
                    dve.wait_ge(s_y, n - RING + 1)
                e = dve.value_load(tile_row[:, bass.ds(n, 1)], min_val=0, max_val=EXPERTS - 1)
                nc.vector.tensor_copy(wbuf[:, b], experts[:, bass.ds(e * BUNDLE, BUNDLE)]).then_inc(s_wcopy, 1)

            def transposed(r, buf):
                dve.wait_ge(s_st, r + 1)
                nc.vector.tensor_scalar(slots_t[:, buf], bank[SLOT_BANKS[buf]][:, 0:ROUND * P], cols_sb[:, 2:3],
                                        cols_sb[:, 3:4], ALU.mult, ALU.add).then_inc(s_slt, 1)

            def expert_round(r, buf):
                transposed(r, buf)
                for b in range(ROUND):
                    fetch((r + 1) * ROUND + b, (1 - buf) * ROUND + b)

            def add_bias(half):
                hs = slice(half * HG, (half + 1) * HG)
                dve.wait_ge(s_hz, half + 1)
                dve.wait_ge(s_b2y, half + 1)
                nc.vector.tensor_tensor(acc[:, hs], bank[BIAS_BANKS[half]][:].rearrange("p (g d) -> p g d", d=D),
                                        acc[:, hs], ALU.add).then_inc(s_accb, 1)

            def combine(half):
                dve.wait_ge(s_accb, half + 1)
                for first in range(0, HG, 2):
                    for k in range(2):
                        for j in (first, first + 1):
                            g = half * HG + j
                            if k == 0:
                                dve.wait_ge(s_back[half][j], 16)
                            else:
                                dve.wait_ge(s_acc[g], 1)
                            nc.vector.scalar_tensor_tensor(acc[:, g], back[:, half, k, j], gate[:, half, k, j:j + 1],
                                                           acc[:, g], ALU.mult, ALU.add).then_inc(s_acc[g], 1)

            embedded(0)
            normalise(n_sb, h_sb, 0, rstd[:, 0], s_norm)
            embedded(1)
            dve.wait_ge(s_const, CONSTS)
            dve.wait_ge(s_vzero, 2)
            spread_q(0)
            normalise(n_sb, h_sb, 1, rstd[:, 0], s_norm)
            spread_v(0)
            below_maximum(0)
            over_sum(0)
            spread_weights(0)
            spread_q(1)
            spread_v(1)
            residual(0)
            twice_normalised(0)
            once_normalised(0)
            below_maximum(1)
            over_sum(1)
            choose(0)
            place(0)
            for e in range(EXPERTS):
                dve.wait_ge(s_w[e], 48)
            dve.wait_ge(s_texp, 1)
            for n in range(RING):
                fetch(n, n, first=True)
            dve.wait_ge(s_cols, 16)
            transposed(0, 0)
            residual(1)
            twice_normalised(1)
            transposed(1, 1)
            once_normalised(1)
            for b in range(ROUND):
                fetch(RING + b, b)
            choose(1)
            transposed(2, 0)
            place(1)
            dve.wait_ge(s_texp, 2)
            fetch(RING + ROUND, ROUND)
            transposed(3, 1)
            for b in range(1, ROUND):
                fetch(RING + ROUND + b, ROUND + b)
            for b in range(ROUND):
                fetch(2 * RING + b, b)
            gates(0)
            gates(1)
            with dve.Fori(2, ROUNDS - 1) as pair:
                expert_round(2 * pair, 0)
                expert_round(2 * pair + 1, 1)
            expert_round(2 * ROUNDS - 2, 0)
            transposed(2 * ROUNDS - 1, 1)
            add_bias(0)
            add_bias(1)
            combine(0)
            combine(1)


def kernel(**inputs):
    import numpy as np
    import concourse.bacc as bacc
    from concourse.bass_utils import run_bass_kernel_spmd

    a = {k: np.asarray(v) for k, v in inputs.items()}
    n_side = IMG // PATCH
    x = a["x"].reshape(BATCH, CHANNELS, n_side, PATCH, n_side, PATCH).transpose(1, 3, 5, 0, 2, 4)
    x = x.reshape(KC, P, GROUPS, P).transpose(1, 2, 0, 3)
    arrays = {
        "x_t": x,
        "w_tok": a["L0_tok_W"].T.reshape(KC, P, D).transpose(1, 0, 2),
        "w_attn": np.stack([a["L0_attn_" + n] for n in ("Wq", "Wk", "Wv", "Wo")]).transpose(1, 0, 2),
        "rows": np.broadcast_to(np.stack([a["L0_tok_b"], a["L0_attn_bv"], a["L0_attn_bo"]]), (P, 3, D)),
        "cols": np.stack([a[n] for n in ("L0_attn_bq", "L0_attn_bk", "L0_ffn_ln_g", "L0_ffn_ln_b")], axis=1),
        "w_router": a["L0_ffn_w_r"].T,
        "b_router": np.broadcast_to(a["L0_ffn_b_r"], (P, EXPERTS)),
        "w1": a["L0_ffn_W1"].transpose(1, 0, 2),
        "b1": a["L0_ffn_b1"].reshape(EXPERTS, FC, P).transpose(2, 0, 1),
        "w2": a["L0_ffn_W2"].reshape(EXPERTS, FC, P, D).transpose(2, 0, 1, 3),
        "b2": a["L0_ffn_b2"],
    }
    arrays = {k: np.ascontiguousarray(v) for k, v in arrays.items()}
    nc = bacc.Bacc("TRN2", target_bir_lowering=False, num_devices=1)
    args = [nc.dram_tensor(f"in_{k}", v.shape, mybir.dt.from_np(v.dtype), kind="ExternalInput").ap()
            for k, v in arrays.items()]
    args += [[nc.dram_tensor(f"{name}{half}", shape, dt, kind="Internal").ap() for half in range(HALVES)]
             for name, shape, dt in (("sorted_x", (TILES * P, D), mybir.dt.float32),
                                     ("slot_ids", (TILES * P, 1), mybir.dt.int32),
                                     ("pair_y", (2 * HT + TILES * P, D), mybir.dt.float32))]
    out = nc.dram_tensor("out_tokens", (P, GROUPS, D), mybir.dt.float32, kind="ExternalOutput").ap()
    vit_tower(nc, *args, out)
    r = run_bass_kernel_spmd(nc, [{f"in_{k}": v for k, v in arrays.items()}], core_ids=[0])
    return r.results[0]["out_tokens"].transpose(1, 0, 2).reshape(BATCH, SEQ, D)
```
